# Optimizing a Trainium2 kernel written in Bass

```python
import numpy as np
import jax
import jax.numpy as jnp

def _softmax(x, axis=-1):
    return jax.nn.softmax(x, axis=axis)
def _gelu(x):
    return jax.nn.gelu(x, approximate=True)
def _silu(x):
    return jax.nn.silu(x)
def _sigmoid(x):
    return jax.nn.sigmoid(x)
def _layernorm(x, axis=-1, eps=1e-5):
    m = jnp.mean(x, axis=axis, keepdims=True)
    v = jnp.var(x, axis=axis, keepdims=True)
    return (x - m) / jnp.sqrt(v + eps)
def _scatter_add(tgt, idx, src, axis=0):
    return tgt.at[idx].add(src)
def _segment_sum(src, seg, n):
    return jax.ops.segment_sum(src, seg, n)

kernel_name = 'mk_conv_seq_d1_conv_nchw512_5f3a53'

def setup_inputs(seed: int = 0):
    np.random.seed(seed)
    _w = jnp.asarray
    def _rec_inputs():
        import jax
        import jax.numpy as jnp
        _gk = jax.random.key(seed)
        x = 7.22e-05 + 1 * jax.random.normal(jax.random.fold_in(_gk, 1), (16, 512, 32, 32), jnp.float32)
        return x
    x = _rec_inputs()
    def _L0_conv_setup():
        import jax, jax.numpy as jnp
        import numpy as np
        import math
        GROUPS = 32
        EPS = 1e-05
        NUM_HEADS = 8

        def group_norm(x, gamma, beta):
            B, C, T = x.shape
            xg = x.reshape(B, GROUPS, C // GROUPS, T)
            mean = xg.mean(axis=(2, 3), keepdims=True)
            var = xg.var(axis=(2, 3), keepdims=True)
            xn = (xg - mean) * jax.lax.rsqrt(var + EPS)
            return xn.reshape(B, C, T) * gamma[None, :, None] + beta[None, :, None]

        def qkv_attention(qkv, num_heads):
            B, C3, T = qkv.shape
            split = C3 // (3 * num_heads)
            q, k, v = jnp.split(qkv, 3, axis=1)
            scale = 1.0 / math.sqrt(math.sqrt(split))
            q = (q * scale).reshape(B * num_heads, split, T)
            k = (k * scale).reshape(B * num_heads, split, T)
            v = v.reshape(B * num_heads, split, T)
            w = jnp.einsum('bct,bcs->bts', q, k)
            w = jax.nn.softmax(w.astype(jnp.float32), axis=-1).astype(w.dtype)
            out = jnp.einsum('bts,bcs->bct', w, v)
            return out.reshape(B, -1, T)
        key = jax.random.key(seed)
        ks = jax.random.split(key, 6)
        B, C, H, W = (16, 512, 32, 32)
        x = jax.random.normal(ks[0], (B, C, H, W), dtype=jnp.float32)
        gamma = jnp.ones((C,), jnp.float32)
        beta = jnp.zeros((C,), jnp.float32)
        w_qkv = jax.random.normal(ks[1], (3 * C, C), jnp.float32) * (1.0 / math.sqrt(C))
        b_qkv = jax.random.normal(ks[2], (3 * C,), jnp.float32) * 0.01
        w_proj = jax.random.normal(ks[3], (C, C), jnp.float32) * (1.0 / math.sqrt(C))
        b_proj = jax.random.normal(ks[4], (C,), jnp.float32) * 0.01
        return {'x': x, 'gamma': gamma, 'beta': beta, 'w_qkv': w_qkv, 'b_qkv': b_qkv, 'w_proj': w_proj, 'b_proj': b_proj}
    _L0_conv_all = _L0_conv_setup()
    _L0_conv_in = {k: v for k, v in _L0_conv_all.items() if k in ('gamma', 'beta', 'w_qkv', 'b_qkv', 'w_proj', 'b_proj', )}
    del _L0_conv_all

    return {
        "x": x,
        "L0_conv_gamma": _L0_conv_in["gamma"],
        "L0_conv_beta": _L0_conv_in["beta"],
        "L0_conv_w_qkv": _L0_conv_in["w_qkv"],
        "L0_conv_b_qkv": _L0_conv_in["b_qkv"],
        "L0_conv_w_proj": _L0_conv_in["w_proj"],
        "L0_conv_b_proj": _L0_conv_in["b_proj"],
    }

def reference(x, L0_conv_gamma, L0_conv_beta, L0_conv_w_qkv, L0_conv_b_qkv, L0_conv_w_proj, L0_conv_b_proj):
    import jax
    import jax.numpy as jnp
    def _L0_conv_ref(x, gamma, beta, w_qkv, b_qkv, w_proj, b_proj):
        import jax, jax.numpy as jnp
        import numpy as np
        import math
        GROUPS = 32
        EPS = 1e-05
        NUM_HEADS = 8

        def group_norm(x, gamma, beta):
            B, C, T = x.shape
            xg = x.reshape(B, GROUPS, C // GROUPS, T)
            mean = xg.mean(axis=(2, 3), keepdims=True)
            var = xg.var(axis=(2, 3), keepdims=True)
            xn = (xg - mean) * jax.lax.rsqrt(var + EPS)
            return xn.reshape(B, C, T) * gamma[None, :, None] + beta[None, :, None]

        def qkv_attention(qkv, num_heads):
            B, C3, T = qkv.shape
            split = C3 // (3 * num_heads)
            q, k, v = jnp.split(qkv, 3, axis=1)
            scale = 1.0 / math.sqrt(math.sqrt(split))
            q = (q * scale).reshape(B * num_heads, split, T)
            k = (k * scale).reshape(B * num_heads, split, T)
            v = v.reshape(B * num_heads, split, T)
            w = jnp.einsum('bct,bcs->bts', q, k)
            w = jax.nn.softmax(w.astype(jnp.float32), axis=-1).astype(w.dtype)
            out = jnp.einsum('bts,bcs->bct', w, v)
            return out.reshape(B, -1, T)
        b, c = (x.shape[0], x.shape[1])
        spatial = x.shape[2:]
        xf = x.reshape(b, c, -1)
        xn = group_norm(xf, gamma, beta)
        qkv = jnp.einsum('oc,bct->bot', w_qkv, xn) + b_qkv[None, :, None]
        h = qkv_attention(qkv, NUM_HEADS)
        h = jnp.einsum('oc,bct->bot', w_proj, h) + b_proj[None, :, None]
        return (xn + h).reshape(b, c, *spatial)

    def _gn(v, G=32, eps=1e-5):
        B_, C_, H_, W_ = v.shape
        g = v.reshape(B_, G, C_ // G, H_, W_)
        m = jnp.mean(g, axis=(2, 3, 4), keepdims=True)
        s = jnp.var(g, axis=(2, 3, 4), keepdims=True)
        return ((g - m) / jnp.sqrt(s + eps)).reshape(v.shape)

    def _ln_c(v, eps=1e-6):
        m = jnp.mean(v, axis=1, keepdims=True)
        s = jnp.var(v, axis=1, keepdims=True)
        return (v - m) / jnp.sqrt(s + eps)

    def _ln_t(v, eps=1e-5):
        m = jnp.mean(v, axis=-1, keepdims=True)
        s = jnp.var(v, axis=-1, keepdims=True)
        return (v - m) / jnp.sqrt(s + eps)

    def _to_tokens(v):
        B_, C_, H_, W_ = v.shape
        return v.reshape(B_, C_, H_ * W_).transpose(0, 2, 1)
    def _from_tokens(t, like):
        B_, C_, H_, W_ = like.shape
        return t.transpose(0, 2, 1).reshape(B_, C_, H_, W_)

    x = _L0_conv_ref(x, L0_conv_gamma, L0_conv_beta, L0_conv_w_qkv, L0_conv_b_qkv, L0_conv_w_proj, L0_conv_b_proj)
    return x


_drawn_inputs = setup_inputs


def setup_inputs(seed=0):
    import zlib

    import numpy as np

    out = dict(_drawn_inputs(seed))
    spreads = {'L0_conv_gamma': (1.0, 0.2), 'L0_conv_beta': (0.0, 0.1)}
    factors = {'L0_conv_b_qkv': 5.983, 'L0_conv_b_proj': 6.11}
    for name, (base, spread) in spreads.items():
        noise = np.random.default_rng([zlib.crc32(name.encode()), seed]).standard_normal(out[name].shape)
        drawn = base * np.exp(spread * noise) if base else spread * noise
        out[name] = jnp.asarray(drawn.astype(out[name].dtype))
    for name, factor in factors.items():
        out[name] = (out[name] * factor).astype(out[name].dtype)
    return out
```

```python
import concourse.bass as bass
from concourse import mybir
from contextlib import ExitStack

B, C, T = 16, 512, 1024
HEADS, D, GROUPS, EPS = 8, 64, 32, 1e-5
P = 128
CT = C // P
PAIRS = HEADS // 2
HALF = T // 2
KT = T // P
STEPS = 2 * KT
LAG = 2
RING = 4
NORM_STEPS = (3, 5, 7, 9)
WS = 16.0
MS = 2048.0


def attention_block_kernel(nc, x, gamma, beta, w_qkv_t, b_qkv, w_proj_t, b_proj, out):
    f32, f16 = mybir.dt.float32, mybir.dt.float16
    ALU = mybir.AluOpType
    ACT = mybir.ActivationFunctionType
    AX = mybir.AxisListType

    x_v = x.rearrange("b (c p) t -> b p c t", p=P)
    out_v = out.rearrange("b (c p) t -> b p c t", p=P)
    wqkv_v = w_qkv_t.rearrange("(c p) o -> p c o", p=P)
    wproj_v = w_proj_t.rearrange("(c p) o -> p c o", p=P)

    ctx = ExitStack()
    with ctx:
        def sb(name, shape, dt):
            return ctx.enter_context(nc.sbuf_tensor(name, shape, dt))

        def pb(name, shape, dt):
            return ctx.enter_context(nc.psum_tensor(name, shape, dt))

        def sem(name):
            return ctx.enter_context(nc.semaphore(name))

        wq_h = sb("wq_h", [P, CT, 3 * C], f16)
        wq_l = sb("wq_l", [P, CT, 3 * C], f16)
        wp_h = sb("wp_h", [P, CT, C], f16)
        wp_l = sb("wp_l", [P, CT, C], f16)
        xn = sb("xn", [P, CT, T], f32)
        resid = sb("resid", [P, CT, T], f32)
        xh = sb("xh", [P, CT, T], f16)
        xl = sb("xl", [P, CT, T], f16)
        nat_h = sb("nat_h", [P, 2, T], f16)
        nat_l = sb("nat_l", [P, 2, T], f16)
        q_cross = sb("q_cross", [P, 2, 2, T], f16)
        k_cross = sb("k_cross", [P, 2, 2, T], f16)
        q_main = sb("q_main", [D + 1, 2, 2, T], f16)
        k_main = sb("k_main", [D + 1, 2, 2, T], f16)
        vh = sb("vh", [P, KT, C], f16)
        vl = sb("vl", [P, KT, C], f16)
        ones = sb("ones", [P, D], f16)
        p32 = sb("p32", [P, 2, 2, HALF], f32)
        ph = sb("ph", [P, RING, 2, HALF], f16)
        pl = sb("pl", [P, RING, 2, HALF], f16)
        inv_sum = sb("inv_sum", [P, HALF], f32)
        att32 = sb("att32", [P, HALF], f32)
        ah = sb("ah", [P, PAIRS, T], f16)
        al = sb("al", [P, PAIRS, T], f16)
        stage = sb("stage", [P, 2, T], f32)
        max_part = sb("max_part", [P, KT, 2, 2], f32)
        max_all = sb("max_all", [P, 2, KT], f32)
        max_row = sb("max_row", [2 * KT, P], f16)
        ident = sb("ident", [P, P], f32)
        group_avg = sb("group_avg", [P, P], f32)
        bq16 = sb("bq16", [P, 3 * CT], f32)
        bias_raw = sb("bias_raw", [P, 3 * CT], f32)
        bproj = sb("bproj", [P, CT], f32)
        gam = sb("gam", [P, CT], f32)
        bet = sb("bet", [P, CT], f32)
        minus_half = sb("minus_half", [P, CT], f32)
        stats = sb("stats", [P, CT, 2, 6], f32)
        mv = sb("mv", [P, CT, 2], f32)
        gmean = sb("gmean", [P, CT], f32)
        dev = sb("dev", [P, CT], f32)
        dev2 = sb("dev2", [P, CT], f32)
        chan_var = sb("chan_var", [P, CT], f32)
        var_eps = sb("var_eps", [P, CT], f32)
        rstd = sb("rstd", [P, CT], f32)
        gn_scale = sb("gn_scale", [P, CT], f32)
        mean_sc = sb("mean_sc", [P, CT], f32)
        gn_shift = sb("gn_shift", [P, CT], f32)

        slots = pb("slots", [P, 2, 2, HALF], f32)
        side = pb("side", [P, 2, HALF], f32)
        acc = pb("acc", [P, HALF], f32)
        sums = pb("sums", [P, HALF], f32)

        w_loaded = [sem(f"w_loaded{i}") for i in range(2)]
        small_loaded = sem("small_loaded")
        w_split_h = sem("w_split_h")
        w_split_l = sem("w_split_l")
        consts_ready = sem("consts_ready")
        rows_ready = sem("rows_ready")
        ident_zero = sem("ident_zero")
        bias_ready = sem("bias_ready")
        x_loaded = [sem(f"x_loaded{c}") for c in range(CT)]
        stats_done = sem("stats_done")
        aggr_done = sem("aggr_done")
        gmean_summed = sem("gmean_summed")
        gmean_copied = sem("gmean_copied")
        dev_done = sem("dev_done")
        dev2_done = sem("dev2_done")
        chan_var_done = sem("chan_var_done")
        gvar_summed = sem("gvar_summed")
        var_eps_done = sem("var_eps_done")
        affine = sem("affine")
        xn_ready = sem("xn_ready")
        xn_done = sem("xn_done")
        xl_done = sem("xl_done")
        resid_done = sem("resid_done")
        qk_summed = sem("qk_summed")
        qk_hi = sem("qk_hi")
        qk_lo = sem("qk_lo")
        stacked = sem("stacked")
        max_tile = sem("max_tile")
        max_reduced = sem("max_reduced")
        max_combined = sem("max_combined")
        max_turned = sem("max_turned")
        max_scaled = sem("max_scaled")
        max_stacked = sem("max_stacked")
        v_summed = sem("v_summed")
        v_hi = sem("v_hi")
        v_lo = sem("v_lo")
        scored = sem("scored")
        exp_done = sem("exp_done")
        ph_done = sem("ph_done")
        pl_done = sem("pl_done")
        pv_done = sem("pv_done")
        inv_done = sem("inv_done")
        acc_read = sem("acc_read")
        att_hi = sem("att_hi")
        att_lo = sem("att_lo")
        proj_summed = sem("proj_summed")
        out_ready = sem("out_ready")
        out_stored = [sem(f"out_stored{i}") for i in range(2)]

        block = ctx.enter_context(nc.Block())

        STACK_DMAS = 12 * 16

        @block.sync
        def _(sp):
            sp.dma_start(bias_raw[:, :], b_qkv).then_inc(small_loaded, 16)
            sp.dma_start(bproj[:, :], b_proj).then_inc(small_loaded, 16)
            sp.dma_start(gam[:, :], gamma).then_inc(small_loaded, 16)
            sp.dma_start(bet[:, :], beta).then_inc(small_loaded, 16)

            for c in range(CT):
                if c >= 2:
                    sp.wait_ge(w_split_l, 2 * (c - 1))
                sp.dma_start(resid[:, 2 * (c % 2):2 * (c % 2) + 2, :].rearrange("p a t -> p (a t)")[:, 0:3 * C],
                             wqkv_v[:, c, :]).then_inc(w_loaded[c % 2], 16)
                sp.dma_start(resid[:, 2 * (c % 2):2 * (c % 2) + 2, :].rearrange("p a t -> p (a t)")[:, 3 * C:4 * C],
                             wproj_v[:, c, :]).then_inc(w_loaded[c % 2], 16)
                sp.dma_start(xn[:, c, :], x_v[0, :, c, :]).then_inc(x_loaded[c], 16)

            def stack_pair(g, par):
                sp.wait_ge(qk_lo, 2 * g + 2)
                for dst, row, src, qk in ((q_cross, 0, nat_h, 0), (q_cross, D, nat_l, 0),
                                          (k_cross, 0, nat_l, 1), (k_cross, D, nat_h, 1),
                                          (q_main, 0, nat_h, 0), (k_main, 0, nat_h, 1)):
                    for h in range(2):
                        sp.dma_start(dst[row:row + D, par, h, :], src[h * D:(h + 1) * D, qk, :]).then_inc(stacked, 16)

            def stack_max(g, par):
                sp.wait_ge(max_scaled, g + 1)
                for h in range(2):
                    sp.dma_start(q_main[D:D + 1, par, h, :].rearrange("o (n t) -> o n t", t=P),
                                 max_row[h * KT:(h + 1) * KT, :]).then_inc(max_stacked, 16)

            stack_pair(0, 0)
            stack_max(0, 0)

            def batch(b, last):
                if not last:
                    for c in range(CT):
                        sp.wait_ge(resid_done, CT * b + c + 1)
                        sp.dma_start(xn[:, c, :], x_v[b + 1, :, c, :]).then_inc(x_loaded[c], 16)
                for p in range(PAIRS):
                    g = b * PAIRS + p
                    if not (last and p == PAIRS - 1):
                        sp.wait_ge(pv_done, STEPS * g)
                        stack_pair(g + 1, (p + 1) % 2)
                        stack_max(g + 1, (p + 1) % 2)
                for j in range(CT):
                    sp.wait_ge(out_ready, CT * b + j + 1)
                    sp.dma_start(out_v[b, :, j, :], stage[:, j % 2, :]).then_inc(out_stored[j % 2], 16)

            batch(0, False)
            with sp.Fori(1, B - 1) as b:
                batch(b, False)
            batch(B - 1, True)
            for i in range(2):
                sp.wait_ge(out_stored[i], 16 * CT // 2 * B)

        @block.gpsimd
        def _(pool):
            nc.gpsimd.memset(ident[:, :], 0.0).then_inc(ident_zero, 1)
            pool.wait_ge(ident_zero, 1)
            nc.gpsimd.affine_select(out=ident[:, :], in_=ident[:, :], compare_op=ALU.not_equal, fill=1.0,
                                    base=0, pattern=[[-1, P]], channel_multiplier=1).then_inc(consts_ready, 1)
            n = C // GROUPS
            nc.gpsimd.memset(group_avg[:, :], 1.0 / n).then_inc(ident_zero, 1)
            pool.wait_ge(ident_zero, 2)
            ga = group_avg[:, :].rearrange("p (g j) -> p g j", j=n)
            nc.gpsimd.affine_select(out=ga, in_=ga, compare_op=ALU.is_ge, fill=0.0,
                                    base=0, pattern=[[-n, P // n], [0, n]], channel_multiplier=1).then_inc(ident_zero, 1)
            pool.wait_ge(ident_zero, 3)
            nc.gpsimd.affine_select(out=ga, in_=ga, compare_op=ALU.is_ge, fill=0.0,
                                    base=n - 1, pattern=[[n, P // n], [0, n]], channel_multiplier=-1).then_inc(consts_ready, 1)
            nc.gpsimd.memset(minus_half[:, :], -0.5).then_inc(ident_zero, 1)
            pool.wait_ge(small_loaded, 64)
            pool.wait_ge(ident_zero, 4)

            def group_norm(nb):
                pool.wait_ge(var_eps_done, nb + 1)
                nc.gpsimd.tensor_tensor(rstd[:, :], var_eps[:, :], minus_half[:, :], ALU.pow).then_inc(affine, 1)
                pool.wait_ge(affine, 4 * nb + 1)
                nc.gpsimd.tensor_tensor(gn_scale[:, :], rstd[:, :], gam[:, :], ALU.mult).then_inc(affine, 1)
                pool.wait_ge(affine, 4 * nb + 2)
                nc.gpsimd.tensor_tensor(mean_sc[:, :], gmean[:, :], gn_scale[:, :], ALU.mult).then_inc(affine, 1)
                pool.wait_ge(affine, 4 * nb + 3)
                nc.gpsimd.tensor_tensor(gn_shift[:, :], bet[:, :], mean_sc[:, :], ALU.subtract).then_inc(affine, 1)
                pool.wait_ge(affine, 4 * nb + 4)
                for c in range(CT):
                    pool.wait_ge(xn_done, CT * nb + c + 1)
                    nc.gpsimd.tensor_tensor(xl[:, c, :], xn[:, c, :], xh[:, c, :], ALU.subtract).then_inc(xl_done, 1)

            group_norm(0)
            with pool.Fori(1, B) as nb:
                group_norm(nb)

        @block.scalar
        def _(act):
            def raw_w(c):
                flat = resid[:, 2 * (c % 2):2 * (c % 2) + 2, :].rearrange("p a t -> p (a t)")
                return flat[:, 0:3 * C], flat[:, 3 * C:4 * C]

            for c in range(CT):
                act.wait_ge(w_loaded[c % 2], 32 * (c // 2 + 1))
                nc.scalar.activation(wq_h[:, c, :], raw_w(c)[0], ACT.Copy, scale=WS).then_inc(w_split_h, 1)
                nc.scalar.activation(wp_h[:, c, :], raw_w(c)[1], ACT.Copy, scale=WS).then_inc(w_split_h, 1)

            def keep_residual(b):
                for c in range(CT):
                    nc.scalar.activation(resid[:, c, :], xn[:, c, :], ACT.Identity,
                                         bias=bproj[:, c:c + 1]).then_inc(resid_done, 1)

            def normalise(nb, c):
                if c == 0:
                    act.wait_ge(affine, 4 * (nb + 1))
                    act.wait_ge(qk_summed, 2 * PAIRS * nb)
                nc.scalar.activation(xn[:, c, :], xn[:, c, :], ACT.Identity, bias=gn_shift[:, c:c + 1],
                                     scale=gn_scale[:, c:c + 1]).then_inc(xn_ready, 1)
                act.wait_ge(xn_ready, CT * nb + c + 1)
                nc.scalar.activation(xh[:, c, :], xn[:, c, :], ACT.Copy).then_inc(xn_done, 1)

            def qk_high(g, p, first=False):
                if not first:
                    act.wait_ge(stacked, STACK_DMAS * g)
                    act.wait_ge(max_tile, STEPS * g)
                for i in range(2):
                    act.wait_ge(qk_summed, 2 * g + i + 1)
                    nc.scalar.activation(nat_h[:, i, :], slots[:, i, :, :].rearrange("p a t -> p (a t)"), ACT.Identity,
                                         bias=bq16[:, i * CT + p:i * CT + p + 1]).then_inc(qk_hi, 1)

            def v_high(nb, first=False):
                if not first:
                    act.wait_ge(pv_done, STEPS * PAIRS * nb)
                for j in range(KT // 2):
                    act.wait_ge(v_summed, 4 * nb + j + 1)
                    nc.scalar.activation(vh[:, 2 * j:2 * j + 2, :], slots[:, j % 2, :, :], ACT.Copy).then_inc(v_hi, 1)

            def attend(g, p, nb):
                for s in range(STEPS):
                    n = g * STEPS + s
                    act.wait_ge(scored, n + 1)
                    if s >= 2:
                        act.wait_ge(pl_done, n - 1)
                    nc.scalar.activation(p32[:, s % 2, :, :], slots[:, s % 2, :, :], ACT.Exp,
                                         scale=1.0 / MS).then_inc(exp_done, 1)
                    act.wait_ge(exp_done, n + 1)
                    if s >= RING:
                        act.wait_ge(pv_done, n - RING + 1)
                    nc.scalar.activation(ph[:, s % RING, :, :], p32[:, s % 2, :, :], ACT.Copy).then_inc(ph_done, 1)
                    if s == KT + LAG:
                        att_high(g, p, 0)
                    if nb is not None and s in NORM_STEPS:
                        normalise(nb, NORM_STEPS.index(s))
                att_high(g, p, 1)

            def att_high(g, p, u):
                act.wait_ge(acc_read, 2 * g + u + 1)
                nc.scalar.activation(ah[:, p, u * HALF:(u + 1) * HALF], att32[:, :], ACT.Identity,
                                     bias=bq16[:, 2 * CT + p:2 * CT + p + 1]).then_inc(att_hi, 1)

            for c in range(CT):
                normalise(0, c)
            act.wait_ge(w_split_l, 2 * CT)
            act.wait_ge(bias_ready, 1)
            qk_high(0, 0, first=True)
            v_high(0, first=True)

            def batch(b, last):
                for p in range(PAIRS):
                    g = b * PAIRS + p
                    if p == 0:
                        act.wait_ge(out_ready, CT * b)
                        keep_residual(b)
                    if not (last and p == PAIRS - 1):
                        qk_high(g + 1, (p + 1) % PAIRS)
                    attend(g, p, b + 1 if p == 2 and not last else None)
                if not last:
                    v_high(b + 1)

            batch(0, False)
            with act.Fori(1, B - 1) as b:
                batch(b, False)
            batch(B - 1, True)

        @block.vector
        def _(dve):
            def raw_w(c):
                flat = resid[:, 2 * (c % 2):2 * (c % 2) + 2, :].rearrange("p a t -> p (a t)")
                return flat[:, 0:3 * C], flat[:, 3 * C:4 * C]

            nc.vector.memset(ones[:, :], 1.0).then_inc(rows_ready, 1)
            nc.vector.memset(k_main[D:D + 1, :, :, :], MS).then_inc(rows_ready, 1)
            dve.wait_ge(small_loaded, 64)
            nc.vector.tensor_scalar(bq16[:, :], bias_raw[:, :], WS, None, ALU.mult).then_inc(bias_ready, 1)
            dve.wait_ge(bias_ready, 1)
            for c in range(CT):
                dve.wait_ge(w_split_h, 2 * c + 2)
                nc.vector.scalar_tensor_tensor(out=wq_l[:, c, :], in0=raw_w(c)[0], scalar=WS, in1=wq_h[:, c, :],
                                               op0=ALU.mult, op1=ALU.subtract).then_inc(w_split_l, 1)
                nc.vector.scalar_tensor_tensor(out=wp_l[:, c, :], in0=raw_w(c)[1], scalar=WS, in1=wp_h[:, c, :],
                                               op0=ALU.mult, op1=ALU.subtract).then_inc(w_split_l, 1)

            def gn_stats(nb, c):
                dve.wait_ge(x_loaded[c], 16 * (nb + 1))
                for a in range(2):
                    nc.vector.bn_stats(stats[:, c, a, :], xn[:, c, a * HALF:(a + 1) * HALF]).then_inc(stats_done, 1)

            def gn_aggr(c):
                nc.vector.bn_aggr(mv[:, c, :], stats[:, c, :, :].rearrange("p a s -> p (a s)")).then_inc(aggr_done, 1)

            def gn_center(nb):
                dve.wait_ge(gmean_summed, nb + 1)
                nc.vector.tensor_copy(gmean[:, :], side[:, 0, 0:CT]).then_inc(gmean_copied, 1)
                dve.wait_ge(gmean_copied, nb + 1)
                nc.vector.tensor_tensor(dev[:, :], mv[:, :, 0], gmean[:, :], ALU.subtract).then_inc(dev_done, 1)
                dve.wait_ge(dev_done, nb + 1)
                nc.vector.tensor_tensor(dev2[:, :], dev[:, :], dev[:, :], ALU.mult).then_inc(dev2_done, 1)
                dve.wait_ge(dev2_done, nb + 1)
                nc.vector.tensor_tensor(chan_var[:, :], dev2[:, :], mv[:, :, 1], ALU.add).then_inc(chan_var_done, 1)

            def gn_var(nb):
                dve.wait_ge(gvar_summed, nb + 1)
                nc.vector.tensor_scalar(var_eps[:, :], side[:, 0, 0:CT], EPS, None, ALU.add).then_inc(var_eps_done, 1)

            def qk_low(g, p, between=None):
                for i in range(2):
                    if i == 1 and between is not None:
                        max_scale(between)
                    dve.wait_ge(qk_hi, 2 * g + i + 1)
                    nc.vector.scalar_tensor_tensor(
                        out=nat_l[:, i, :], in0=slots[:, i, :, :].rearrange("p a t -> p (a t)"),
                        scalar=bq16[:, i * CT + p:i * CT + p + 1], in1=nat_h[:, i, :],
                        op0=ALU.add, op1=ALU.subtract).then_inc(qk_lo, 1)

            def v_low(nb, between=None):
                for j in range(KT // 2):
                    if j == 1 and between is not None:
                        max_scale(between)
                    dve.wait_ge(v_hi, 4 * nb + j + 1)
                    nc.vector.tensor_tensor(vl[:, 2 * j:2 * j + 2, :], slots[:, j % 2, :, :], vh[:, 2 * j:2 * j + 2, :],
                                            ALU.subtract).then_inc(v_lo, 1)

            def max_reduce(g, m):
                dve.wait_ge(max_tile, g * STEPS + m + 1)
                nc.vector.tensor_reduce(max_part[:, m // 2, m % 2, :], side[:, :, :], axis=AX.X,
                                        op=ALU.max).then_inc(max_reduced, 1)

            def max_combine(g):
                dve.wait_ge(max_reduced, (g + 1) * STEPS)
                nc.vector.tensor_tensor(max_all[:, :, :].rearrange("p h n -> p n h"), max_part[:, :, 0, :],
                                        max_part[:, :, 1, :], ALU.max).then_inc(max_combined, 1)

            def max_scale(g, first=False):
                dve.wait_ge(max_turned, g + 1)
                if not first:
                    dve.wait_ge(max_stacked, 32 * g)
                nc.vector.tensor_scalar(max_row[:, :], side[0:2 * KT, 0, 0:P], -1.0 / MS, None,
                                        ALU.mult).then_inc(max_scaled, 1)

            def finish_half(g, p, u):
                dve.wait_ge(pv_done, g * STEPS + (u + 1) * KT)
                nc.vector.reciprocal(inv_sum[:, :], sums[:, :]).then_inc(inv_done, 1)
                dve.wait_ge(inv_done, 2 * g + u + 1)
                dve.wait_ge(att_hi, 2 * g + u)
                nc.vector.tensor_tensor(att32[:, :], acc[:, :], inv_sum[:, :], ALU.mult).then_inc(acc_read, 1)

            def att_low(g, p, u):
                dve.wait_ge(att_hi, 2 * g + u + 1)
                cols = slice(u * HALF, (u + 1) * HALF)
                nc.vector.scalar_tensor_tensor(out=al[:, p, cols], in0=att32[:, :],
                                               scalar=bq16[:, 2 * CT + p:2 * CT + p + 1], in1=ah[:, p, cols],
                                               op0=ALU.add, op1=ALU.subtract).then_inc(att_lo, 1)

            def attend(g, p, next_pair, nb):
                aggregate = nb is not None and p == 0
                for s in range(STEPS):
                    n = g * STEPS + s
                    if aggregate and s and s % CT == 0:
                        dve.wait_ge(stats_done, 2 * (CT * nb + s // CT))
                    if next_pair:
                        max_reduce(g + 1, s)
                    if aggregate and s and s % CT == 0:
                        gn_aggr(s // CT - 1)
                    if s == KT + LAG - 1:
                        finish_half(g, p, 0)
                    dve.wait_ge(ph_done, n + 1)
                    if s >= RING:
                        dve.wait_ge(pv_done, n - RING + 1)
                    nc.vector.tensor_tensor(pl[:, s % RING, :, :], p32[:, s % 2, :, :], ph[:, s % RING, :, :],
                                            ALU.subtract).then_inc(pl_done, 1)
                    if s == KT + LAG + 1:
                        att_low(g, p, 0)
                    if aggregate and s % CT == CT - 1:
                        gn_stats(nb, s // CT)
                if aggregate:
                    dve.wait_ge(stats_done, 2 * CT * (nb + 1))
                if next_pair:
                    max_combine(g + 1)
                if aggregate:
                    gn_aggr(CT - 1)
                finish_half(g, p, 1)
                att_low(g, p, 1)

            def project(b):
                for j in range(CT):
                    dve.wait_ge(proj_summed, CT * b + j + 1)
                    dve.wait_ge(out_stored[j % 2], 16 * (CT // 2 * b + j // 2))
                    if j == 0:
                        dve.wait_ge(resid_done, CT * (b + 1))
                    nc.vector.scalar_tensor_tensor(
                        out=stage[:, j % 2, :], in0=slots[:, j % 2, :, :].rearrange("p a t -> p (a t)"),
                        scalar=1.0 / (WS * WS), in1=resid[:, j, :], op0=ALU.mult, op1=ALU.add).then_inc(out_ready, 1)

            for c in range(CT):
                gn_stats(0, c)
                dve.wait_ge(stats_done, 2 * (c + 1))
                gn_aggr(c)
            gn_center(0)
            gn_var(0)
            qk_low(0, 0)
            v_low(0)
            for m in range(STEPS):
                max_reduce(0, m)
            max_combine(0)
            max_scale(0, first=True)

            def batch(b, last):
                for p in range(PAIRS):
                    g = b * PAIRS + p
                    next_pair = not (last and p == PAIRS - 1)
                    if next_pair:
                        qk_low(g + 1, (p + 1) % PAIRS, g if p > 0 else None)
                    else:
                        max_scale(g)
                    if p == 1 and not last:
                        gn_center(b + 1)
                    if p == 2 and not last:
                        gn_var(b + 1)
                    attend(g, p, next_pair, None if last else b + 1)
                if not last:
                    v_low(b + 1, PAIRS * (b + 1))
                project(b)

            batch(0, False)
            with dve.Fori(1, B - 1) as b:
                batch(b, False)
            batch(B - 1, True)

        @block.tensor
        def _(pe):
            mm = nc.tensor.matmul
            pe.wait_ge(consts_ready, 2)
            pe.wait_ge(rows_ready, 2)

            def gn_group_mean(nb):
                pe.wait_ge(aggr_done, CT * (nb + 1))
                mm(side[:, 0, 0:CT], group_avg[:, :], mv[:, :, 0], start=True, stop=True).then_inc(gmean_summed, 1)

            def gn_group_var(nb):
                pe.wait_ge(chan_var_done, nb + 1)
                mm(side[:, 0, 0:CT], group_avg[:, :], chan_var[:, :], start=True, stop=True).then_inc(gvar_summed, 1)

            def three(bank, parts):
                last = None
                terms = [(w[i], m[j]) for w, m in parts for i, j in ((0, 0), (0, 1), (1, 0))]
                for t, (w, m) in enumerate(terms):
                    last = mm(bank, w, m, start=t == 0, stop=t == len(terms) - 1)
                return last

            def qk_project(g, p, between=None):
                for i in range(2):
                    if i == 1 and between is not None:
                        max_turn(between)
                    cols = slice(i * C + p * P, i * C + (p + 1) * P)
                    for a in range(2):
                        last = three(slots[:, i, a, :], [((wq_h[:, c, cols], wq_l[:, c, cols]),
                                                             (xh[:, c, a * HALF:(a + 1) * HALF], xl[:, c, a * HALF:(a + 1) * HALF]))
                                                            for c in range(CT)])
                    last.then_inc(qk_summed, 1)

            def v_project(nb, free, between=None):
                for j in range(KT // 2):
                    if j == 1 and between is not None:
                        max_turn(between)
                    if j < 2:
                        free(j)
                    else:
                        pe.wait_ge(v_lo, 4 * nb + j - 1)
                    for a in range(2):
                        pos = slice((2 * j + a) * P, (2 * j + a + 1) * P)
                        last = three(slots[:, j % 2, a, :], [((xh[:, c, pos], xl[:, c, pos]),
                                                                 (wq_h[:, c, 2 * C:3 * C], wq_l[:, c, 2 * C:3 * C]))
                                                                for c in range(CT)])
                    last.then_inc(v_summed, 1)

            def max_pass(g, m):
                if m == 0:
                    pe.wait_ge(qk_hi, 2 * g + 2)
                pe.wait_ge(max_reduced, g * STEPS + m)
                q0, k0 = (m // 2) * P, (m % 2) * HALF
                for h in range(2):
                    last = mm(side[:, h, :], nat_h[h * D:(h + 1) * D, 0, q0:q0 + P],
                              nat_h[h * D:(h + 1) * D, 1, k0:k0 + HALF], start=True, stop=True)
                last.then_inc(max_tile, 1)

            def max_turn(g):
                pe.wait_ge(max_combined, g + 1)
                nc.tensor.transpose(side[0:2 * KT, 0, 0:P], max_all[:, :, :].rearrange("p h n -> p (h n)"),
                                    ident[:, :]).then_inc(max_turned, 1)

            def score(g, par, s, free):
                n = g * STEPS + s
                if s < 2:
                    free(s)
                else:
                    pe.wait_ge(exp_done, n - 1)
                if s == 0:
                    pe.wait_ge(stacked, STACK_DMAS * (g + 1))
                    pe.wait_ge(max_stacked, 32 * (g + 1))
                u, st = s // KT, s % KT
                keys, queries = slice(st * P, (st + 1) * P), slice(u * HALF, (u + 1) * HALF)
                for h in range(2):
                    mm(slots[:, s % 2, h, :], k_cross[:, par, h, keys], q_cross[:, par, h, queries], start=True, stop=False)
                    last = mm(slots[:, s % 2, h, :], k_main[:, par, h, keys], q_main[:, par, h, queries], start=False, stop=True)
                last.then_inc(scored, 1)

            def weigh(g, p, s):
                n = g * STEPS + s
                u, st = s // KT, s % KT
                pe.wait_ge(pl_done, n + 1)
                if st == 0:
                    pe.wait_ge(acc_read, 2 * g + u)
                first, end = st == 0, st == KT - 1
                r = s % RING
                for i, (v, m) in enumerate(((vh, ph), (vl, ph), (vh, pl))):
                    for h in range(2):
                        c0 = p * P + h * D
                        mm(acc[h * D:(h + 1) * D, :], v[:, st, c0:c0 + D], m[:, r, h, :],
                           start=first and i == 0, stop=end and i == 2)
                for i, m in enumerate((ph, pl)):
                    for h in range(2):
                        last = mm(sums[h * D:(h + 1) * D, :], ones[:, :], m[:, r, h, :],
                                  start=first and i == 0, stop=end and i == 1)
                last.then_inc(pv_done, 1)

            def attend(g, p, next_pair, free):
                for s in range(STEPS + LAG):
                    if s < STEPS:
                        score(g, p % 2, s, free)
                        if next_pair:
                            if s == 0:
                                pe.wait_ge(max_scaled, g + 1)
                            max_pass(g + 1, s)
                    if s >= LAG:
                        weigh(g, p, s - LAG)

            def project(b, free):
                for j in range(CT):
                    if j == 0:
                        pe.wait_ge(att_lo, 2 * PAIRS * (b + 1))
                    if j < 2:
                        free(j)
                    else:
                        pe.wait_ge(out_ready, CT * b + j - 1)
                    cols = slice(j * P, (j + 1) * P)
                    for a in range(2):
                        half = slice(a * HALF, (a + 1) * HALF)
                        last = three(slots[:, j % 2, a, :], [((wp_h[:, c, cols], wp_l[:, c, cols]),
                                                                 (ah[:, c, half], al[:, c, half])) for c in range(PAIRS)])
                    last.then_inc(proj_summed, 1)

            gn_group_mean(0)
            pe.wait_ge(gmean_copied, 1)
            gn_group_var(0)
            pe.wait_ge(w_split_l, 2 * CT)
            pe.wait_ge(xl_done, CT)
            qk_project(0, 0)
            v_project(0, lambda j: pe.wait_ge(qk_lo, j + 1))
            pe.wait_ge(var_eps_done, 1)
            for m in range(STEPS):
                max_pass(0, m)
            max_turn(0)

            def batch(b, last):
                for p in range(PAIRS):
                    g = b * PAIRS + p
                    next_pair = not (last and p == PAIRS - 1)
                    if p == 0:
                        pe.wait_ge(v_lo, 4 * (b + 1))
                        pe.wait_ge(out_ready, CT * b)
                    else:
                        pe.wait_ge(exp_done, g * STEPS)
                    if next_pair:
                        if p == PAIRS - 1:
                            pe.wait_ge(xl_done, CT * (b + 2))
                        qk_project(g + 1, (p + 1) % PAIRS, g if p > 0 else None)
                    else:
                        max_turn(g)
                    if p == 1 and not last:
                        pe.wait_ge(max_scaled, g + 1)
                        gn_group_mean(b + 1)
                    if p == 2 and not last:
                        pe.wait_ge(max_scaled, g + 1)
                        gn_group_var(b + 1)
                    if p == 1 and not last:
                        pe.wait_ge(gmean_copied, b + 2)
                    if p == 2 and not last:
                        pe.wait_ge(var_eps_done, b + 2)
                    attend(g, p, next_pair,
                           (lambda j: pe.wait_ge(qk_lo, 2 * (g + 1) + j + 1)) if next_pair
                           else (lambda j: None))
                done = (b + 1) * PAIRS * STEPS
                if last:
                    project(b, lambda j: pe.wait_ge(exp_done, done + j - 1))
                else:
                    v_project(b + 1, lambda j: pe.wait_ge(exp_done, done + j - 1), PAIRS * (b + 1))
                    project(b, lambda j: pe.wait_ge(v_lo, 4 * (b + 1) + 3 + j))

            batch(0, False)
            with pe.Fori(1, B - 1) as b:
                batch(b, False)
            batch(B - 1, True)


def kernel(**inputs):
    import numpy as _np
    import concourse.bacc as _bacc
    from concourse import mybir as _mybir
    from concourse.bass_utils import run_bass_kernel_spmd as _run

    nc = _bacc.Bacc("TRN2", target_bir_lowering=False, num_devices=1)
    f = {k: _np.asarray(v) for k, v in inputs.items()}
    laid_out = {
        "x": f["x"].reshape(B, C, T),
        "gamma": f["L0_conv_gamma"].reshape(-1, P).T,
        "beta": f["L0_conv_beta"].reshape(-1, P).T,
        "w_qkv_t": _np.ascontiguousarray(f["L0_conv_w_qkv"].T),
        "b_qkv": f["L0_conv_b_qkv"].reshape(-1, P).T,
        "w_proj_t": _np.ascontiguousarray(f["L0_conv_w_proj"].T),
        "b_proj": f["L0_conv_b_proj"].reshape(-1, P).T,
    }
    arrays, args = {}, []
    for name, a in laid_out.items():
        a = _np.ascontiguousarray(a)
        arrays[name] = a
        args.append(nc.dram_tensor(name, a.shape, _mybir.dt.from_np(a.dtype), kind="ExternalInput").ap())
    y = nc.dram_tensor("y", (B, C, T), _mybir.dt.float32, kind="ExternalOutput").ap()
    attention_block_kernel(nc, *args, y)
    r = _run(nc, [arrays], core_ids=[0])
    return r.results[0]["y"].reshape(f["x"].shape)
```

```python
import concourse.bass as bass
from concourse import mybir
from contextlib import ExitStack

B, C, T = 16, 512, 1024
HEADS, D, GROUPS, EPS = 8, 64, 32, 1e-5
P = 128
CT = C // P
PAIRS = HEADS // 2
HALF = T // 2
KT = T // P
STEPS = 2 * KT
QUARTER = HALF // 2
RING = 4
NORM_STEPS = (5, 7, 9, 11)
WS = 16.0
MS = 2048.0


def attention_block_kernel(nc, x, gamma, beta, w_qkv_t, b_qkv, w_proj_t, b_proj, out):
    f32, f16 = mybir.dt.float32, mybir.dt.float16
    ALU = mybir.AluOpType
    ACT = mybir.ActivationFunctionType
    AX = mybir.AxisListType

    x_v = x.rearrange("b (c p) t -> b p c t", p=P)
    out_v = out.rearrange("b (c p) t -> b p c t", p=P)
    wqkv_v = w_qkv_t.rearrange("(c p) o -> p c o", p=P)
    wproj_v = w_proj_t.rearrange("(c p) o -> p c o", p=P)

    ctx = ExitStack()
    with ctx:
        def sb(name, shape, dt):
            return ctx.enter_context(nc.sbuf_tensor(name, shape, dt))

        def pb(name, shape, dt):
            return ctx.enter_context(nc.psum_tensor(name, shape, dt))

        def sem(name):
            return ctx.enter_context(nc.semaphore(name))

        wq_h = sb("wq_h", [P, CT, 3 * C], f16)
        wq_l = sb("wq_l", [P, CT, 3 * C], f16)
        wp_h = sb("wp_h", [P, CT, C], f16)
        wp_l = sb("wp_l", [P, CT, C], f16)
        x_sb = sb("x_sb", [P, CT, T], f32)
        resid = sb("resid", [P, CT, T], f32)
        xh = sb("xh", [P, CT, T], f16)
        xl = sb("xl", [P, CT, T], f16)
        xn32 = sb("xn32", [P, 2, T], f32)
        nat_h = sb("nat_h", [P, 2, T], f16)
        nat_l = sb("nat_l", [P, 2, T], f16)
        q_cross = sb("q_cross", [P, 2, 2, T], f16)
        k_cross = sb("k_cross", [P, 2, 2, T], f16)
        q_main = sb("q_main", [D + 1, 2, 2, T], f16)
        k_main = sb("k_main", [D + 1, 2, 2, T], f16)
        vh = sb("vh", [P, KT, C], f16)
        vl = sb("vl", [P, KT, C], f16)
        ones = sb("ones", [P, D], f16)
        p32 = sb("p32", [P, 2, 2, HALF], f32)
        ph = sb("ph", [P, RING, 2, HALF], f16)
        pl = sb("pl", [P, RING, 2, HALF], f16)
        sums_sb = sb("sums_sb", [P, 2, QUARTER], f32)
        inv_sum = sb("inv_sum", [P, 2, QUARTER], f32)
        inv_all = sb("inv_all", [P, 2, HALF], f32)
        att32 = sb("att32", [P, 2, HALF], f32)
        ah = sb("ah", [P, PAIRS, T], f16)
        al = sb("al", [P, PAIRS, T], f16)
        stage = sb("stage", [P, 2, T], f32)
        max_part = sb("max_part", [P, KT, 2, 2], f32)
        max_all = sb("max_all", [P, 2, KT], f32)
        max_row = sb("max_row", [2 * KT, P], f16)
        ident = sb("ident", [P, P], f32)
        group_avg = sb("group_avg", [P, P], f32)
        bq16 = sb("bq16", [P, 3 * CT], f32)
        bias_raw = sb("bias_raw", [P, 3 * CT], f32)
        bv_h = sb("bv_h", [P, CT], f16)
        bv_l = sb("bv_l", [P, CT], f16)
        bproj_raw = sb("bproj_raw", [P, CT], f32)
        bproj = sb("bproj", [P, CT], f32)
        gam = sb("gam", [P, CT], f32)
        bet = sb("bet", [P, CT], f32)
        minus_half = sb("minus_half", [P, CT], f32)
        stats = sb("stats", [P, CT, 2, 6], f32)
        mv = sb("mv", [P, CT, 2], f32)
        gmean = sb("gmean", [P, CT], f32)
        dev = sb("dev", [P, CT], f32)
        dev2 = sb("dev2", [P, CT], f32)
        chan_var = sb("chan_var", [P, CT], f32)
        var_eps = sb("var_eps", [P, CT], f32)
        rstd = sb("rstd", [P, CT], f32)
        gn_scale = sb("gn_scale", [P, CT], f32)
        mean_sc = sb("mean_sc", [P, CT], f32)
        gn_shift = sb("gn_shift", [P, CT], f32)
        resid_shift = sb("resid_shift", [P, CT], f32)

        slots = pb("slots", [P, 2, 2, HALF], f32)
        side = pb("side", [P, 2, HALF], f32)
        acc = pb("acc", [P, HALF], f32)
        sums = pb("sums", [P, HALF], f32)

        w_loaded = [sem(f"w_loaded{i}") for i in range(2)]
        small_loaded = sem("small_loaded")
        x_loaded = [sem(f"x_loaded{c}") for c in range(CT)]
        w_split_h = sem("w_split_h")
        w_split_l = sem("w_split_l")
        consts_ready = sem("consts_ready")
        rows_ready = sem("rows_ready")
        bias_ready = sem("bias_ready")
        bv_split = sem("bv_split")
        bv_summed = sem("bv_summed")
        bproj_ready = sem("bproj_ready")
        stats_done = sem("stats_done")
        aggr_done = sem("aggr_done")
        gmean_summed = sem("gmean_summed")
        gmean_copied = sem("gmean_copied")
        dev_done = sem("dev_done")
        dev2_done = sem("dev2_done")
        chan_var_done = sem("chan_var_done")
        gvar_summed = sem("gvar_summed")
        var_eps_done = sem("var_eps_done")
        affine = sem("affine")
        resid_shifted = sem("resid_shifted")
        xh_done = sem("xh_done")
        xn_done = sem("xn_done")
        xl_done = sem("xl_done")
        resid_done = sem("resid_done")
        qk_summed = sem("qk_summed")
        qk_hi = sem("qk_hi")
        qk_lo = sem("qk_lo")
        stacked = sem("stacked")
        v_summed = sem("v_summed")
        v_hi = sem("v_hi")
        v_lo = sem("v_lo")
        max_tile = sem("max_tile")
        max_reduced = sem("max_reduced")
        max_combined = sem("max_combined")
        max_turned = sem("max_turned")
        max_scaled = sem("max_scaled")
        max_stacked = sem("max_stacked")
        scored = sem("scored")
        exp_done = sem("exp_done")
        ph_done = sem("ph_done")
        pl_done = sem("pl_done")
        pv_done = sem("pv_done")
        half_read = sem("half_read")
        inv_done = sem("inv_done")
        inv_spread = [sem(f"inv_spread{u}") for u in range(2)]
        att_scaled = sem("att_scaled")
        att_hi = sem("att_hi")
        att_lo = sem("att_lo")
        proj_summed = sem("proj_summed")
        out_ready = sem("out_ready")
        out_stored = [sem(f"out_stored{i}") for i in range(2)]

        block = ctx.enter_context(nc.Block())

        STACKED = 12 * 16
        SPREAD = 8 * 16

        def raw_w(c):
            flat = resid[:, 2 * (c % 2):2 * (c % 2) + 2, :].rearrange("p a t -> p (a t)")
            return flat[:, 0:3 * C], flat[:, 3 * C:4 * C]

        def two_banks(t):
            return t.rearrange("p a t -> p (a t)")


        @block.sync
        def _(sp):
            sp.dma_start(bias_raw[:, :], b_qkv).then_inc(small_loaded, 16)
            sp.dma_start(bproj_raw[:, :], b_proj).then_inc(small_loaded, 16)
            sp.dma_start(gam[:, :], gamma).then_inc(small_loaded, 16)
            sp.dma_start(bet[:, :], beta).then_inc(small_loaded, 16)
            for c in range(CT):
                sp.dma_start(x_sb[:, c, :], x_v[0, :, c, :]).then_inc(x_loaded[c], 16)
            for c in range(CT):
                if c >= 2:
                    sp.wait_ge(w_split_l, 2 * (c - 1))
                sp.dma_start(raw_w(c)[0], wqkv_v[:, c, :]).then_inc(w_loaded[c % 2], 16)
                sp.dma_start(raw_w(c)[1], wproj_v[:, c, :]).then_inc(w_loaded[c % 2], 16)

            def stack_pair(g, par):
                sp.wait_ge(qk_lo, 2 * g + 2)
                for dst, row, src, qk in ((q_cross, 0, nat_h, 0), (q_cross, D, nat_l, 0),
                                          (k_cross, 0, nat_l, 1), (k_cross, D, nat_h, 1),
                                          (q_main, 0, nat_h, 0), (k_main, 0, nat_h, 1)):
                    for h in range(2):
                        sp.dma_start(dst[row:row + D, par, h, :], src[h * D:(h + 1) * D, qk, :]).then_inc(stacked, 16)

            def stack_max(g, par):
                sp.wait_ge(max_scaled, g + 1)
                for h in range(2):
                    sp.dma_start(q_main[D:D + 1, par, h, :].rearrange("o (n t) -> o n t", t=P),
                                 max_row[h * KT:(h + 1) * KT, :]).then_inc(max_stacked, 16)

            def spread_inverses(g):
                for u in range(2):
                    sp.wait_ge(inv_done, 2 * g + u + 1)
                    for h in range(2):
                        for q in range(2):
                            for k in range(2):
                                src = 32 * (2 * h + q)
                                dst = 32 * (2 * h + k)
                                sp.dma_start(inv_all[dst:dst + 32, u, q * QUARTER:(q + 1) * QUARTER],
                                             inv_sum[src:src + 32, u, :]).then_inc(inv_spread[u], 16)

            def store_out(b):
                for j in range(CT):
                    sp.wait_ge(out_ready, CT * b + j + 1)
                    sp.dma_start(out_v[b, :, j, :], stage[:, j % 2, :]).then_inc(out_stored[j % 2], 16)

            def turn(b, before, after, p, first, last):
                g = b * PAIRS + p
                stack_max(g, p % 2)
                if not (first and p == 0):
                    spread_inverses(g - 1)
                if p == 0 and not first:
                    store_out(before)
                if not (last and p == PAIRS - 1):
                    if not (first and p == 0):
                        sp.wait_ge(scored, STEPS * g)
                    stack_pair(g + 1, (p + 1) % 2)
                if p == 1 and not last:
                    for c in range(CT):
                        sp.wait_ge(resid_done, CT * b + c + 1)
                        sp.dma_start(x_sb[:, c, :], x_v[after, :, c, :]).then_inc(x_loaded[c], 16)

            stack_pair(0, 0)
            for p in range(PAIRS):
                turn(0, None, 1, p, True, False)
            with sp.Fori(1, B - 1) as b:
                before, after = sp.snap(b - 1), sp.snap(b + 1)
                for p in range(PAIRS):
                    turn(b, before, after, p, False, False)
            for p in range(PAIRS):
                turn(B - 1, B - 2, None, p, False, True)
            spread_inverses(B * PAIRS - 1)
            store_out(B - 1)
            for i in range(2):
                sp.wait_ge(out_stored[i], 16 * CT // 2 * B)

        @block.gpsimd
        def _(pool):
            nc.gpsimd.memset(ident[:, :], 0.0).then_inc(consts_ready, 1)
            pool.wait_ge(consts_ready, 1)
            nc.gpsimd.affine_select(out=ident[:, :], in_=ident[:, :], compare_op=ALU.not_equal, fill=1.0,
                                    base=0, pattern=[[-1, P]], channel_multiplier=1).then_inc(consts_ready, 1)
            n = C // GROUPS
            nc.gpsimd.memset(group_avg[:, :], 1.0 / n).then_inc(consts_ready, 1)
            pool.wait_ge(consts_ready, 3)
            ga = group_avg[:, :].rearrange("p (g j) -> p g j", j=n)
            nc.gpsimd.affine_select(out=ga, in_=ga, compare_op=ALU.is_ge, fill=0.0,
                                    base=0, pattern=[[-n, P // n], [0, n]], channel_multiplier=1).then_inc(consts_ready, 1)
            pool.wait_ge(consts_ready, 4)
            nc.gpsimd.affine_select(out=ga, in_=ga, compare_op=ALU.is_ge, fill=0.0,
                                    base=n - 1, pattern=[[n, P // n], [0, n]], channel_multiplier=-1).then_inc(consts_ready, 1)
            nc.gpsimd.memset(minus_half[:, :], -0.5).then_inc(consts_ready, 1)
            pool.wait_ge(small_loaded, 64)
            pool.wait_ge(consts_ready, 6)

            def group_norm(nb, first=False):
                tt = nc.gpsimd.tensor_tensor
                if not first:
                    pool.wait_ge(xl_done, CT * nb)
                pool.wait_ge(var_eps_done, nb + 1)
                tt(rstd[:, :], var_eps[:, :], minus_half[:, :], ALU.pow).then_inc(affine, 1)
                pool.wait_ge(affine, 4 * nb + 1)
                tt(gn_scale[:, :], rstd[:, :], gam[:, :], ALU.mult).then_inc(affine, 1)
                pool.wait_ge(affine, 4 * nb + 2)
                tt(mean_sc[:, :], gmean[:, :], gn_scale[:, :], ALU.mult).then_inc(affine, 1)
                pool.wait_ge(affine, 4 * nb + 3)
                tt(gn_shift[:, :], bet[:, :], mean_sc[:, :], ALU.subtract).then_inc(affine, 1)

                def full(c):
                    nc.gpsimd.tensor_scalar(xn32[:, c % 2, :], x_sb[:, c, :], gn_scale[:, c:c + 1], gn_shift[:, c:c + 1],
                                            ALU.mult, ALU.add).then_inc(xn_done, 1)

                def low(c):
                    pool.wait_ge(xh_done, CT * nb + c + 1)
                    pool.wait_ge(xn_done, CT * nb + c + 1)
                    if c:
                        pool.wait_ge(xl_done, CT * nb + c)
                    tt(xl[:, c, :], xn32[:, c % 2, :], xh[:, c, :], ALU.subtract).then_inc(xl_done, 1)

                def shift_residual():
                    tt(resid_shift[:, :], gn_shift[:, :], bproj[:, :], ALU.add).then_inc(resid_shifted, 1)

                pool.wait_ge(affine, 4 * nb + 4)
                if not first:
                    shift_residual()
                full(0)
                full(1)
                low(0)
                for c in range(1, CT):
                    low(c)
                    if c + 1 < CT:
                        full(c + 1)
                if first:
                    pool.wait_ge(bproj_ready, 1)
                    shift_residual()

            def finish_pair(g, p):
                tt = nc.gpsimd.tensor_tensor
                halves = [slice(u * HALF, (u + 1) * HALF) for u in range(2)]
                for u in range(2):
                    pool.wait_ge(inv_spread[u], SPREAD * (g + 1))
                    tt(ah[:, p, halves[u]], att32[:, u, :], inv_all[:, u, :], ALU.mult).then_inc(att_hi, 1)
                for u in range(2):
                    pool.wait_ge(att_hi, 2 * g + u + 1)
                    tt(att32[:, u, :], att32[:, u, :], inv_all[:, u, :], ALU.mult).then_inc(att_scaled, 1)
                for u in range(2):
                    pool.wait_ge(att_scaled, 2 * g + u + 1)
                    tt(al[:, p, halves[u]], att32[:, u, :], ah[:, p, halves[u]], ALU.subtract).then_inc(att_lo, 1)

            def turn(b, p, first, last):
                if p == 1 and not first:
                    pool.wait_ge(proj_summed, CT * b)
                if not (first and p == 0):
                    finish_pair(b * PAIRS + p - 1, (p - 1) % PAIRS)
                if p == 2 and not last:
                    group_norm(b + 1)

            group_norm(0, first=True)
            for p in range(PAIRS):
                turn(0, p, True, False)
            with pool.Fori(1, B - 1) as b:
                for p in range(PAIRS):
                    turn(b, p, False, False)
            for p in range(PAIRS):
                turn(B - 1, p, False, True)
            finish_pair(B * PAIRS - 1, PAIRS - 1)

        @block.scalar
        def _(act):
            def normalise(nb, c):
                if c == 0:
                    act.wait_ge(affine, 4 * (nb + 1))
                    act.wait_ge(qk_summed, 2 * PAIRS * nb)
                nc.scalar.activation(xh[:, c, :], x_sb[:, c, :], ACT.Identity, bias=gn_shift[:, c:c + 1],
                                     scale=gn_scale[:, c:c + 1]).then_inc(xh_done, 1)

            def make_residual(b, c):
                nc.scalar.activation(resid[:, c, :], x_sb[:, c, :], ACT.Identity, bias=resid_shift[:, c:c + 1],
                                     scale=gn_scale[:, c:c + 1]).then_inc(resid_done, 1)

            def qk_high(g, i, p, first=False):
                if i == 0 and not first:
                    act.wait_ge(stacked, STACKED * g)
                    act.wait_ge(max_tile, STEPS * g)
                act.wait_ge(qk_summed, 2 * g + i + 1)
                src = slots[:, 0, :, :] if i == 0 else side[:, :, :]
                nc.scalar.activation(nat_h[:, i, :], two_banks(src), ACT.Identity,
                                     bias=bq16[:, i * CT + p:i * CT + p + 1]).then_inc(qk_hi, 1)

            def v_high(b):
                for j in range(KT // 2):
                    act.wait_ge(v_summed, 4 * b + j + 1)
                    nc.scalar.activation(vh[:, 2 * j:2 * j + 2, :], slots[:, j % 2, :, :], ACT.Copy).then_inc(v_hi, 1)

            def numerators(g, s):
                n = g * STEPS + s
                act.wait_ge(scored, n + 1)
                if s >= 2:
                    act.wait_ge(pl_done, n - 1)
                nc.scalar.activation(p32[:, s % 2, :, :], slots[:, s % 2, :, :], ACT.Exp,
                                     scale=1.0 / MS).then_inc(exp_done, 1)
                act.wait_ge(exp_done, n + 1)
                if s >= RING:
                    act.wait_ge(pv_done, n - RING + 1)
                nc.scalar.activation(ph[:, s % RING, :, :], p32[:, s % 2, :, :], ACT.Copy).then_inc(ph_done, 1)

            def read_half(g, u, first=False):
                act.wait_ge(pv_done, g * STEPS + (u + 1) * KT)
                if not first:
                    act.wait_ge(att_lo, 2 * g)
                nc.scalar.activation(att32[:, u, :], acc[:, :], ACT.Copy)
                nc.scalar.activation(sums_sb[:, u, :], sums[:, 0:QUARTER], ACT.Copy).then_inc(half_read, 1)

            def turn(b, p, first, last):
                g = b * PAIRS + p
                has_next = not (last and p == PAIRS - 1)
                if not (first and p == 0):
                    read_half(g - 1, 1, first=first and p == 1)
                if has_next:
                    qk_high(g + 1, 0, (p + 1) % PAIRS)
                if p == 0:
                    v_high(b)
                if p == 1:
                    if not first:
                        act.wait_ge(out_ready, CT * b)
                    act.wait_ge(resid_shifted, b + 1)
                    for c in range(CT):
                        make_residual(b, c)
                numerators(g, 0)
                numerators(g, 1)
                if has_next:
                    qk_high(g + 1, 1, (p + 1) % PAIRS)
                for s in range(2, STEPS):
                    numerators(g, s)
                    if s == KT + 1:
                        read_half(g, 0, first=first and p == 0)
                    if p == 2 and not last and s in NORM_STEPS:
                        normalise(b + 1, NORM_STEPS.index(s))

            for c in range(CT):
                normalise(0, c)
            for c in range(CT):
                act.wait_ge(w_loaded[c % 2], 32 * (c // 2 + 1))
                nc.scalar.activation(wq_h[:, c, :], raw_w(c)[0], ACT.Copy, scale=WS).then_inc(w_split_h, 1)
                nc.scalar.activation(wp_h[:, c, :], raw_w(c)[1], ACT.Copy, scale=WS).then_inc(w_split_h, 1)
            act.wait_ge(bias_ready, 1)
            qk_high(0, 0, 0, first=True)
            qk_high(0, 1, 0)
            act.wait_ge(w_split_l, 2 * CT)
            for p in range(PAIRS):
                turn(0, p, True, False)
            with act.Fori(1, B - 1) as b:
                for p in range(PAIRS):
                    turn(b, p, False, False)
            for p in range(PAIRS):
                turn(B - 1, p, False, True)
            read_half(B * PAIRS - 1, 1)

        @block.vector
        def _(dve):
            nc.vector.memset(ones[:, :], 1.0).then_inc(rows_ready, 1)
            nc.vector.memset(k_main[D:D + 1, :, :, :], MS).then_inc(rows_ready, 1)
            dve.wait_ge(small_loaded, 64)
            nc.vector.tensor_scalar(bq16[:, :], bias_raw[:, :], WS, None, ALU.mult).then_inc(bias_ready, 1)
            dve.wait_ge(bias_ready, 1)
            nc.vector.tensor_copy(bv_h[:, :], bq16[:, 2 * CT:3 * CT]).then_inc(bv_split, 1)
            dve.wait_ge(bv_split, 1)
            nc.vector.tensor_tensor(bv_l[:, :], bq16[:, 2 * CT:3 * CT], bv_h[:, :], ALU.subtract).then_inc(bv_split, 1)

            def gn_stats(nb, c):
                dve.wait_ge(x_loaded[c], 16 * (nb + 1))
                for a in range(2):
                    nc.vector.bn_stats(stats[:, c, a, :], x_sb[:, c, a * HALF:(a + 1) * HALF]).then_inc(stats_done, 1)

            def gn_aggregate():
                for c in range(CT):
                    nc.vector.bn_aggr(mv[:, c, :], stats[:, c, :, :].rearrange("p a s -> p (a s)")).then_inc(aggr_done, 1)

            def gn_center(nb):
                dve.wait_ge(gmean_summed, nb + 1)
                nc.vector.tensor_copy(gmean[:, :], acc[:, 0:CT]).then_inc(gmean_copied, 1)
                dve.wait_ge(gmean_copied, nb + 1)
                nc.vector.tensor_tensor(dev[:, :], mv[:, :, 0], gmean[:, :], ALU.subtract).then_inc(dev_done, 1)
                dve.wait_ge(dev_done, nb + 1)
                nc.vector.tensor_tensor(dev2[:, :], dev[:, :], dev[:, :], ALU.mult).then_inc(dev2_done, 1)
                dve.wait_ge(dev2_done, nb + 1)
                nc.vector.tensor_tensor(chan_var[:, :], dev2[:, :], mv[:, :, 1], ALU.add).then_inc(chan_var_done, 1)

            def gn_var(nb):
                dve.wait_ge(gvar_summed, nb + 1)
                nc.vector.tensor_scalar(var_eps[:, :], acc[:, 0:CT], EPS, None, ALU.add).then_inc(var_eps_done, 1)

            def qk_low(g, i, p):
                dve.wait_ge(qk_hi, 2 * g + i + 1)
                src = slots[:, 0, :, :] if i == 0 else side[:, :, :]
                nc.vector.scalar_tensor_tensor(
                    out=nat_l[:, i, :], in0=two_banks(src), scalar=bq16[:, i * CT + p:i * CT + p + 1],
                    in1=nat_h[:, i, :], op0=ALU.add, op1=ALU.subtract).then_inc(qk_lo, 1)

            def v_low(b):
                for j in range(KT // 2):
                    dve.wait_ge(v_hi, 4 * b + j + 1)
                    nc.vector.tensor_tensor(vl[:, 2 * j:2 * j + 2, :], slots[:, j % 2, :, :], vh[:, 2 * j:2 * j + 2, :],
                                            ALU.subtract).then_inc(v_lo, 1)

            def max_reduce(g, m):
                dve.wait_ge(max_tile, g * STEPS + m + 1)
                nc.vector.tensor_reduce(max_part[:, m // 2, m % 2, :], side[:, :, :], axis=AX.X,
                                        op=ALU.max).then_inc(max_reduced, 1)

            def max_combine(g):
                dve.wait_ge(max_reduced, (g + 1) * STEPS)
                nc.vector.tensor_tensor(max_all[:, :, :].rearrange("p h n -> p n h"), max_part[:, :, 0, :],
                                        max_part[:, :, 1, :], ALU.max).then_inc(max_combined, 1)

            def max_finish(g, first=False):
                dve.wait_ge(max_turned, g + 1)
                if not first:
                    dve.wait_ge(max_stacked, 32 * g)
                nc.vector.tensor_scalar(max_row[:, :], side[0:2 * KT, 0, 0:P], -1.0 / MS, None,
                                        ALU.mult).then_inc(max_scaled, 1)

            def low_numerators(g, s):
                n = g * STEPS + s
                dve.wait_ge(ph_done, n + 1)
                if s >= RING:
                    dve.wait_ge(pv_done, n - RING + 1)
                nc.vector.tensor_tensor(pl[:, s % RING, :, :], p32[:, s % 2, :, :], ph[:, s % RING, :, :],
                                        ALU.subtract).then_inc(pl_done, 1)

            def invert(g, u, first=False):
                dve.wait_ge(half_read, 2 * g + u + 1)
                if not first:
                    dve.wait_ge(inv_spread[u], SPREAD * g)
                nc.vector.reciprocal(inv_sum[:, u, :], sums_sb[:, u, :]).then_inc(inv_done, 1)

            def project(b, first=False):
                for j in range(CT):
                    dve.wait_ge(proj_summed, CT * b + j + 1)
                    if j >= 2 or not first:
                        dve.wait_ge(out_stored[j % 2], 16 * (CT // 2 * b + j // 2))
                    if j == 0:
                        dve.wait_ge(resid_done, CT * (b + 1))
                    nc.vector.scalar_tensor_tensor(
                        out=stage[:, j % 2, :], in0=two_banks(slots[:, j % 2, :, :]),
                        scalar=1.0 / (WS * WS), in1=resid[:, j, :], op0=ALU.mult, op1=ALU.add).then_inc(out_ready, 1)

            def turn(b, p, first, last):
                g = b * PAIRS + p
                has_next = not (last and p == PAIRS - 1)
                start = first and p == 0
                norm = p == 2 and not last
                if not start:
                    invert(g - 1, 0, first=first and p == 1)
                max_reduce(g, STEPS - 2)
                if norm:
                    gn_stats(b + 1, 0)
                max_reduce(g, STEPS - 1)
                max_combine(g)
                if norm:
                    gn_stats(b + 1, 1)
                max_finish(g, first=start)
                if norm:
                    gn_stats(b + 1, 2)
                    gn_stats(b + 1, 3)
                if not start and not norm:
                    invert(g - 1, 1, first=first and p == 1)
                if norm:
                    dve.wait_ge(stats_done, 2 * CT * (b + 2))
                if has_next:
                    qk_low(g + 1, 0, (p + 1) % PAIRS)
                if norm:
                    gn_aggregate()
                    invert(g - 1, 1)
                if p == 0:
                    v_low(b)
                    if not first:
                        project(b - 1, first=isinstance(b, int) and b == 1)
                if norm:
                    gn_center(b + 1)
                low_numerators(g, 0)
                if norm:
                    gn_var(b + 1)
                low_numerators(g, 1)
                if has_next:
                    qk_low(g + 1, 1, (p + 1) % PAIRS)
                for s in range(2, STEPS):
                    if has_next:
                        max_reduce(g + 1, s - 2)
                    low_numerators(g, s)

            for c in range(CT):
                gn_stats(0, c)
            dve.wait_ge(stats_done, 2 * CT)
            gn_aggregate()
            gn_center(0)
            gn_var(0)
            for c in range(CT):
                dve.wait_ge(w_split_h, 2 * c + 2)
                nc.vector.scalar_tensor_tensor(out=wq_l[:, c, :], in0=raw_w(c)[0], scalar=WS, in1=wq_h[:, c, :],
                                               op0=ALU.mult, op1=ALU.subtract).then_inc(w_split_l, 1)
                nc.vector.scalar_tensor_tensor(out=wp_l[:, c, :], in0=raw_w(c)[1], scalar=WS, in1=wp_h[:, c, :],
                                               op0=ALU.mult, op1=ALU.subtract).then_inc(w_split_l, 1)
            dve.wait_ge(bv_summed, 1)
            nc.vector.scalar_tensor_tensor(out=bproj[:, :], in0=acc[:, 0:CT], scalar=1.0 / (WS * WS), in1=bproj_raw[:, :],
                                           op0=ALU.mult, op1=ALU.add).then_inc(bproj_ready, 1)
            qk_low(0, 0, 0)
            qk_low(0, 1, 0)
            for m in range(STEPS - 2):
                max_reduce(0, m)
            for p in range(PAIRS):
                turn(0, p, True, False)
            with dve.Fori(1, B - 1) as b:
                for p in range(PAIRS):
                    turn(b, p, False, False)
            for p in range(PAIRS):
                turn(B - 1, p, False, True)
            invert(B * PAIRS - 1, 0)
            invert(B * PAIRS - 1, 1)
            project(B - 1)

        @block.tensor
        def _(pe):
            mm = nc.tensor.matmul
            pe.wait_ge(consts_ready, 6)
            pe.wait_ge(rows_ready, 2)

            def gn_group_mean(nb):
                pe.wait_ge(aggr_done, CT * (nb + 1))
                mm(acc[:, 0:CT], group_avg[:, :], mv[:, :, 0], start=True, stop=True).then_inc(gmean_summed, 1)

            def gn_group_var(nb):
                pe.wait_ge(chan_var_done, nb + 1)
                mm(acc[:, 0:CT], group_avg[:, :], chan_var[:, :], start=True, stop=True).then_inc(gvar_summed, 1)

            def three(bank, parts, midway=None):
                last = None
                terms = [(w[i], m[j]) for w, m in parts for i, j in ((0, 0), (0, 1), (1, 0))]
                for t, (w, m) in enumerate(terms):
                    if midway and t == len(terms) // 2:
                        midway()
                    last = mm(bank, w, m, start=t == 0, stop=t == len(terms) - 1)
                return last

            def qk_project(i, a, p, midway=None):
                cols = slice(i * C + p * P, i * C + (p + 1) * P)
                half = slice(a * HALF, (a + 1) * HALF)
                bank = slots[:, 0, a, :] if i == 0 else side[:, a, :]
                last = three(bank, [((wq_h[:, c, cols], wq_l[:, c, cols]), (xh[:, c, half], xl[:, c, half]))
                                    for c in range(CT)], midway)
                if a == 1:
                    last.then_inc(qk_summed, 1)

            def v_project(b, free):
                for j in range(KT // 2):
                    if j < 2:
                        free(j)
                    else:
                        pe.wait_ge(v_lo, 4 * b + j - 1)
                    for a in range(2):
                        pos = slice((2 * j + a) * P, (2 * j + a + 1) * P)
                        last = three(slots[:, j % 2, a, :], [((xh[:, c, pos], xl[:, c, pos]),
                                                              (wq_h[:, c, 2 * C:3 * C], wq_l[:, c, 2 * C:3 * C]))
                                                             for c in range(CT)])
                    last.then_inc(v_summed, 1)

            def max_pass(g, m):
                if m == 0:
                    pe.wait_ge(qk_lo, 2 * g + 2)
                else:
                    pe.wait_ge(max_reduced, g * STEPS + m)
                q0, k0 = (m // 2) * P, (m % 2) * HALF
                for h in range(2):
                    last = mm(side[:, h, :], nat_h[h * D:(h + 1) * D, 0, q0:q0 + P],
                              nat_h[h * D:(h + 1) * D, 1, k0:k0 + HALF], start=True, stop=True)
                last.then_inc(max_tile, 1)

            def max_turn(g):
                pe.wait_ge(max_combined, g + 1)
                nc.tensor.transpose(side[0:2 * KT, 0, 0:P], max_all[:, :, :].rearrange("p h n -> p (h n)"),
                                    ident[:, :]).then_inc(max_turned, 1)

            def score(g, par, s):
                if s >= 2:
                    pe.wait_ge(exp_done, g * STEPS + s - 1)
                u, st = s // KT, s % KT
                keys, queries = slice(st * P, (st + 1) * P), slice(u * HALF, (u + 1) * HALF)
                for h in range(2):
                    mm(slots[:, s % 2, h, :], k_cross[:, par, h, keys], q_cross[:, par, h, queries], start=True, stop=False)
                    last = mm(slots[:, s % 2, h, :], k_main[:, par, h, keys], q_main[:, par, h, queries], start=False, stop=True)
                last.then_inc(scored, 1)

            def weigh(g, p, s):
                u, st = s // KT, s % KT
                pe.wait_ge(pl_done, g * STEPS + s + 1)
                for i, (v, m) in enumerate(((vh, ph), (vl, ph), (vh, pl))):
                    for h in range(2):
                        c0 = p * P + h * D
                        mm(acc[h * D:(h + 1) * D, :], v[:, st, c0:c0 + D], m[:, s % RING, h, :],
                           start=st == 0 and i == 0, stop=st == KT - 1 and i == 2)

            def add_up(s):
                st = s % KT
                for i, m in enumerate((ph, pl)):
                    for h in range(2):
                        for q in range(2):
                            row = 32 * (2 * h + q)
                            last = mm(sums[row:row + 32, 0:QUARTER], ones[:, 0:32],
                                      m[:, s % RING, h, q * QUARTER:(q + 1) * QUARTER],
                                      start=st == 0 and i == 0, stop=st == KT - 1 and i == 1)
                last.then_inc(pv_done, 1)

            def project(b, free):
                for j in range(CT):
                    if j == 0:
                        pe.wait_ge(att_lo, 2 * PAIRS * (b + 1))
                    if j < 2:
                        free(j)
                    else:
                        pe.wait_ge(out_ready, CT * b + j - 1)
                    cols = slice(j * P, (j + 1) * P)
                    for a in range(2):
                        half = slice(a * HALF, (a + 1) * HALF)
                        last = three(slots[:, j % 2, a, :], [((wp_h[:, c, cols], wp_l[:, c, cols]),
                                                              (ah[:, c, half], al[:, c, half])) for c in range(PAIRS)])
                    last.then_inc(proj_summed, 1)

            def turn(b, p, first, last):
                g = b * PAIRS + p
                has_next = not (last and p == PAIRS - 1)
                start = first and p == 0
                norm = p == 2 and not last
                if has_next:
                    if p == PAIRS - 1:
                        pe.wait_ge(xl_done, CT * (b + 2))
                    if not start:
                        pe.wait_ge(exp_done, STEPS * g - 1)
                    qk_project(0, 0, (p + 1) % PAIRS)
                max_pass(g, STEPS - 2)
                if not start:
                    weigh(g - 1, (p - 1) % PAIRS, STEPS - 2)
                    weigh(g - 1, (p - 1) % PAIRS, STEPS - 1)
                max_pass(g, STEPS - 1)
                if not start:
                    add_up(STEPS - 2)
                    add_up(STEPS - 1)
                if has_next:
                    qk_project(0, 1, (p + 1) % PAIRS, midway=lambda: max_turn(g))
                else:
                    max_turn(g)
                if p == 0:
                    def slot_for_v(j):
                        if j == 0:
                            pe.wait_ge(qk_lo, 2 * (g + 1) + 1)
                        elif not start:
                            pe.wait_ge(exp_done, STEPS * g)
                    v_project(b, slot_for_v)
                if has_next:
                    pe.wait_ge(max_scaled, g + 1)
                    qk_project(1, 0, (p + 1) % PAIRS)
                if p == 0 and not first:
                    project(b - 1, lambda j: pe.wait_ge(v_lo, 4 * b + 3 + j))
                pe.wait_ge(stacked, STACKED * (g + 1))
                pe.wait_ge(max_stacked, 32 * (g + 1))
                if p == 0:
                    pe.wait_ge(v_lo, 4 * (b + 1))
                    if not first:
                        pe.wait_ge(out_ready, CT * b)
                elif has_next:
                    pe.wait_ge(qk_lo, 2 * (g + 1) + 1)
                    pe.wait_ge(exp_done, STEPS * g)
                else:
                    pe.wait_ge(exp_done, STEPS * g)
                score(g, p % 2, 0)
                score(g, p % 2, 1)
                if norm:
                    pe.wait_ge(half_read, 2 * g)
                    gn_group_mean(b + 1)
                if has_next:
                    qk_project(1, 1, (p + 1) % PAIRS)
                if norm:
                    gn_group_var(b + 1)
                for s in range(2, STEPS, 2):
                    score(g, p % 2, s)
                    score(g, p % 2, s + 1)
                    if has_next and s > 2:
                        max_pass(g + 1, s - 2)
                    if norm and s == 2:
                        pe.wait_ge(var_eps_done, b + 2)
                    if s == 2 and not start:
                        pe.wait_ge(half_read, 2 * g)
                    if s == KT + 2:
                        pe.wait_ge(half_read, 2 * g + 1)
                    weigh(g, p, s - 2)
                    weigh(g, p, s - 1)
                    if has_next and s == 2:
                        max_pass(g + 1, 0)
                    elif has_next:
                        max_pass(g + 1, s - 1)
                    add_up(s - 2)
                    add_up(s - 1)
                    if has_next and s == 2:
                        max_pass(g + 1, 1)

            gn_group_mean(0)
            gn_group_var(0)
            pe.wait_ge(w_split_l, 2 * CT)
            pe.wait_ge(var_eps_done, 1)
            pe.wait_ge(bv_split, 2)
            for j in range(CT):
                cols = slice(j * P, (j + 1) * P)
                last = three(acc[:, j:j + 1], [((wp_h[:, c, cols], wp_l[:, c, cols]),
                                                (bv_h[:, c:c + 1], bv_l[:, c:c + 1])) for c in range(CT)])
            last.then_inc(bv_summed, 1)
            pe.wait_ge(xl_done, CT)
            for i in range(2):
                for a in range(2):
                    qk_project(i, a, 0)
            for m in range(STEPS - 2):
                max_pass(0, m)
            pe.wait_ge(qk_lo, 2)
            pe.wait_ge(bproj_ready, 1)
            for p in range(PAIRS):
                turn(0, p, True, False)
            with pe.Fori(1, B - 1) as b:
                for p in range(PAIRS):
                    turn(b, p, False, False)
            for p in range(PAIRS):
                turn(B - 1, p, False, True)
            g_end = B * PAIRS
            for s in (STEPS - 2, STEPS - 1):
                weigh(g_end - 1, PAIRS - 1, s)
            for s in (STEPS - 2, STEPS - 1):
                add_up(s)
            project(B - 1, lambda j: pe.wait_ge(exp_done, STEPS * g_end - 1 + j))


def kernel(**inputs):
    import numpy as _np
    import concourse.bacc as _bacc
    from concourse import mybir as _mybir
    from concourse.bass_utils import run_bass_kernel_spmd as _run

    nc = _bacc.Bacc("TRN2", target_bir_lowering=False, num_devices=1)
    f = {k: _np.asarray(v) for k, v in inputs.items()}
    laid_out = {
        "x": f["x"].reshape(B, C, T),
        "gamma": f["L0_conv_gamma"].reshape(-1, P).T,
        "beta": f["L0_conv_beta"].reshape(-1, P).T,
        "w_qkv_t": _np.ascontiguousarray(f["L0_conv_w_qkv"].T),
        "b_qkv": f["L0_conv_b_qkv"].reshape(-1, P).T,
        "w_proj_t": _np.ascontiguousarray(f["L0_conv_w_proj"].T),
        "b_proj": f["L0_conv_b_proj"].reshape(-1, P).T,
    }
    arrays, args = {}, []
    for name, a in laid_out.items():
        a = _np.ascontiguousarray(a)
        arrays[name] = a
        args.append(nc.dram_tensor(name, a.shape, _mybir.dt.from_np(a.dtype), kind="ExternalInput").ap())
    y = nc.dram_tensor("y", (B, C, T), _mybir.dt.float32, kind="ExternalOutput").ap()
    attention_block_kernel(nc, *args, y)
    r = _run(nc, [arrays], core_ids=[0])
    return r.results[0]["y"].reshape(f["x"].shape)
```

```python
import concourse.bass as bass
from concourse import mybir
from contextlib import ExitStack

B, C, T = 16, 512, 1024
HEADS, D, GROUPS, EPS = 8, 64, 32, 1e-5
P = 128
CT = C // P
PAIRS = HEADS // 2
HALF = T // 2
KT = T // P
STEPS = 2 * KT
QUARTER = HALF // 2
RING = 4
POOL_STEPS = (1, 5, 9, 13)
WS = 16.0
MS = 2048.0


def attention_block_kernel(nc, x, gamma, beta, w_qkv_t, b_qkv, w_proj_t, b_proj, out):
    f32, f16 = mybir.dt.float32, mybir.dt.float16
    ALU = mybir.AluOpType
    ACT = mybir.ActivationFunctionType
    AX = mybir.AxisListType

    x_v = x.rearrange("b (c p) t -> b p c t", p=P)
    out_v = out.rearrange("b (c p) t -> b p c t", p=P)
    wqkv_v = w_qkv_t.rearrange("(c p) o -> p c o", p=P)
    wproj_v = w_proj_t.rearrange("(c p) o -> p c o", p=P)

    ctx = ExitStack()
    with ctx:
        def sb(name, shape, dt):
            return ctx.enter_context(nc.sbuf_tensor(name, shape, dt))

        def pb(name, shape, dt):
            return ctx.enter_context(nc.psum_tensor(name, shape, dt))

        def sem(name):
            return ctx.enter_context(nc.semaphore(name))

        wq_h = sb("wq_h", [P, CT, 3 * C], f16)
        wq_l = sb("wq_l", [P, CT, 3 * C], f16)
        wp_h = sb("wp_h", [P, CT, C], f16)
        wp_l = sb("wp_l", [P, CT, C], f16)
        x_sb = sb("x_sb", [P, CT, T], f32)
        resid = sb("resid", [P, CT, T], f32)
        xh = sb("xh", [P, CT, T], f16)
        xl = sb("xl", [P, CT, T], f16)
        xn32 = sb("xn32", [P, 2, T], f32)
        nat_h = sb("nat_h", [P, 2, T], f16)
        nat_l = sb("nat_l", [P, 2, T], f16)
        q_cross = sb("q_cross", [P, 2, 2, T], f16)
        k_cross = sb("k_cross", [P, 2, 2, T], f16)
        q_main = sb("q_main", [D + 1, 2, 2, T], f16)
        k_main = sb("k_main", [D + 1, 2, 2, T], f16)
        vh = sb("vh", [P, KT, C], f16)
        vl = sb("vl", [P, KT, C], f16)
        ones = sb("ones", [P, D], f16)
        p32 = sb("p32", [P, 2, 2, HALF], f32)
        ph = sb("ph", [P, RING, 2, HALF], f16)
        pl = sb("pl", [P, RING, 2, HALF], f16)
        sums_sb = sb("sums_sb", [P, 2, QUARTER], f32)
        inv_sum = sb("inv_sum", [P, 2, QUARTER], f32)
        inv_all = sb("inv_all", [P, 2, HALF], f32)
        att32 = sb("att32", [P, 2, HALF], f32)
        ah = sb("ah", [P, PAIRS, T], f16)
        al = sb("al", [P, PAIRS, T], f16)
        stage = sb("stage", [P, 2, T], f32)
        max_part = sb("max_part", [P, KT, 2, 2], f32)
        max_all = sb("max_all", [P, 2, KT], f32)
        max_row = sb("max_row", [2 * KT, P], f16)
        ident = sb("ident", [P, P], f32)
        group_avg = sb("group_avg", [P, P], f32)
        bq16 = sb("bq16", [P, 3 * CT], f32)
        bias_raw = sb("bias_raw", [P, 3 * CT], f32)
        bv_h = sb("bv_h", [P, CT], f16)
        bv_l = sb("bv_l", [P, CT], f16)
        bproj_raw = sb("bproj_raw", [P, CT], f32)
        bproj = sb("bproj", [P, CT], f32)
        gam = sb("gam", [P, CT], f32)
        bet = sb("bet", [P, CT], f32)
        minus_half = sb("minus_half", [P, CT], f32)
        stats = sb("stats", [P, CT, 2, 6], f32)
        mv = sb("mv", [P, CT, 2], f32)
        gmean = sb("gmean", [P, CT], f32)
        dev = sb("dev", [P, CT], f32)
        dev2 = sb("dev2", [P, CT], f32)
        chan_var = sb("chan_var", [P, CT], f32)
        var_eps = sb("var_eps", [P, CT], f32)
        rstd = sb("rstd", [P, CT], f32)
        gn_scale = sb("gn_scale", [P, CT], f32)
        mean_sc = sb("mean_sc", [P, CT], f32)
        gn_shift = sb("gn_shift", [P, CT], f32)
        resid_shift = sb("resid_shift", [P, CT], f32)

        slots = pb("slots", [P, 2, 2, HALF], f32)
        side = pb("side", [P, 2, HALF], f32)
        acc = pb("acc", [P, HALF], f32)
        sums = pb("sums", [P, HALF], f32)

        w_loaded = [sem(f"w_loaded{i}") for i in range(2)]
        small_loaded = sem("small_loaded")
        x_loaded = [sem(f"x_loaded{c}") for c in range(CT)]
        w_split_h = sem("w_split_h")
        w_split_l = sem("w_split_l")
        consts_ready = sem("consts_ready")
        rows_ready = sem("rows_ready")
        bias_ready = sem("bias_ready")
        bv_split = sem("bv_split")
        bv_summed = sem("bv_summed")
        bproj_ready = sem("bproj_ready")
        stats_done = sem("stats_done")
        aggr_done = sem("aggr_done")
        gmean_summed = sem("gmean_summed")
        gmean_copied = sem("gmean_copied")
        dev_done = sem("dev_done")
        dev2_done = sem("dev2_done")
        chan_var_done = sem("chan_var_done")
        gvar_summed = sem("gvar_summed")
        var_eps_done = sem("var_eps_done")
        affine = sem("affine")
        resid_shifted = sem("resid_shifted")
        xh_done = sem("xh_done")
        xn_done = sem("xn_done")
        xl_done = sem("xl_done")
        resid_done = sem("resid_done")
        q_summed = sem("q_summed")
        k_summed = sem("k_summed")
        q_hi = sem("q_hi")
        k_hi = sem("k_hi")
        qk_lo = sem("qk_lo")
        stacked = sem("stacked")
        v_summed = sem("v_summed")
        v_hi = sem("v_hi")
        v_lo = sem("v_lo")
        max_tile = sem("max_tile")
        max_reduced = sem("max_reduced")
        max_combined = sem("max_combined")
        max_turned = sem("max_turned")
        max_scaled = sem("max_scaled")
        max_stacked = sem("max_stacked")
        scored = sem("scored")
        exp_done = sem("exp_done")
        ph_done = sem("ph_done")
        pl_done = sem("pl_done")
        pool_pl_done = sem("pool_pl_done")
        pv_done = sem("pv_done")
        half_read = sem("half_read")
        inv_done = sem("inv_done")
        inv_spread = [sem(f"inv_spread{u}") for u in range(2)]
        att_scaled = sem("att_scaled")
        att_hi = sem("att_hi")
        att_lo = sem("att_lo")
        proj_summed = sem("proj_summed")
        out_ready = sem("out_ready")
        out_stored = [sem(f"out_stored{i}") for i in range(2)]

        block = ctx.enter_context(nc.Block())

        STACKED = 12 * 16
        SPREAD = 8 * 16

        def wait_low(engine, g, s):
            mine = sum(t in POOL_STEPS for t in range(s + 1))
            if s in POOL_STEPS:
                engine.wait_ge(pool_pl_done, len(POOL_STEPS) * g + mine)
            else:
                engine.wait_ge(pl_done, (STEPS - len(POOL_STEPS)) * g + s + 1 - mine)

        def raw_w(c):
            flat = resid[:, 2 * (c % 2):2 * (c % 2) + 2, :].rearrange("p a t -> p (a t)")
            return flat[:, 0:3 * C], flat[:, 3 * C:4 * C]

        def two_banks(t):
            return t.rearrange("p a t -> p (a t)")


        @block.sync
        def _(sp):
            sp.dma_start(bias_raw[:, :], b_qkv).then_inc(small_loaded, 16)
            sp.dma_start(bproj_raw[:, :], b_proj).then_inc(small_loaded, 16)
            sp.dma_start(gam[:, :], gamma).then_inc(small_loaded, 16)
            sp.dma_start(bet[:, :], beta).then_inc(small_loaded, 16)
            for c in range(CT):
                sp.dma_start(x_sb[:, c, :], x_v[0, :, c, :]).then_inc(x_loaded[c], 16)
            for c in range(CT):
                if c >= 2:
                    sp.wait_ge(w_split_l, 2 * (c - 1))
                sp.dma_start(raw_w(c)[0], wqkv_v[:, c, :]).then_inc(w_loaded[c % 2], 16)
                sp.dma_start(raw_w(c)[1], wproj_v[:, c, :]).then_inc(w_loaded[c % 2], 16)

            def stack_pair(g, par):
                sp.wait_ge(qk_lo, 2 * g + 2)
                for dst, row, src, qk in ((q_cross, 0, nat_h, 0), (q_cross, D, nat_l, 0),
                                          (k_cross, 0, nat_l, 1), (k_cross, D, nat_h, 1),
                                          (q_main, 0, nat_h, 0), (k_main, 0, nat_h, 1)):
                    for h in range(2):
                        sp.dma_start(dst[row:row + D, par, h, :], src[h * D:(h + 1) * D, qk, :]).then_inc(stacked, 16)

            def stack_max(g, par):
                sp.wait_ge(max_scaled, g + 1)
                for h in range(2):
                    sp.dma_start(q_main[D:D + 1, par, h, :].rearrange("o (n t) -> o n t", t=P),
                                 max_row[h * KT:(h + 1) * KT, :]).then_inc(max_stacked, 16)

            def spread_inverses(g, u):
                sp.wait_ge(inv_done, 2 * g + u + 1)
                for h in range(2):
                    for q in range(2):
                        for k in range(2):
                            src = 32 * (2 * h + q)
                            dst = 32 * (2 * h + k)
                            sp.dma_start(inv_all[dst:dst + 32, u, q * QUARTER:(q + 1) * QUARTER],
                                         inv_sum[src:src + 32, u, :]).then_inc(inv_spread[u], 16)

            def store_out(b):
                for j in range(CT):
                    sp.wait_ge(out_ready, CT * b + j + 1)
                    sp.dma_start(out_v[b, :, j, :], stage[:, j % 2, :]).then_inc(out_stored[j % 2], 16)

            def turn(b, before, after, p, first, last):
                g = b * PAIRS + p
                norm = p == 2 and not last
                if norm:
                    spread_inverses(g - 1, 0)
                stack_max(g, p % 2)
                if not (first and p == 0):
                    for u in (1,) if norm else (0, 1):
                        spread_inverses(g - 1, u)
                if p == 0 and not first:
                    store_out(before)
                if not (last and p == PAIRS - 1):
                    if not (first and p == 0):
                        sp.wait_ge(scored, STEPS * g)
                    stack_pair(g + 1, (p + 1) % 2)
                if p == 1 and not last:
                    for c in range(CT):
                        sp.wait_ge(resid_done, CT * b + c + 1)
                        sp.dma_start(x_sb[:, c, :], x_v[after, :, c, :]).then_inc(x_loaded[c], 16)

            stack_pair(0, 0)
            for p in range(PAIRS):
                turn(0, None, 1, p, True, False)
            with sp.Fori(1, B - 1) as b:
                before, after = sp.snap(b - 1), sp.snap(b + 1)
                for p in range(PAIRS):
                    turn(b, before, after, p, False, False)
            for p in range(PAIRS):
                turn(B - 1, B - 2, None, p, False, True)
            spread_inverses(B * PAIRS - 1, 0)
            spread_inverses(B * PAIRS - 1, 1)
            store_out(B - 1)
            for i in range(2):
                sp.wait_ge(out_stored[i], 16 * CT // 2 * B)

        @block.gpsimd
        def _(pool):
            nc.gpsimd.memset(ident[:, :], 0.0).then_inc(consts_ready, 1)
            pool.wait_ge(consts_ready, 1)
            nc.gpsimd.affine_select(out=ident[:, :], in_=ident[:, :], compare_op=ALU.not_equal, fill=1.0,
                                    base=0, pattern=[[-1, P]], channel_multiplier=1).then_inc(consts_ready, 1)
            n = C // GROUPS
            nc.gpsimd.memset(group_avg[:, :], 1.0 / n).then_inc(consts_ready, 1)
            pool.wait_ge(consts_ready, 3)
            ga = group_avg[:, :].rearrange("p (g j) -> p g j", j=n)
            nc.gpsimd.affine_select(out=ga, in_=ga, compare_op=ALU.is_ge, fill=0.0,
                                    base=0, pattern=[[-n, P // n], [0, n]], channel_multiplier=1).then_inc(consts_ready, 1)
            pool.wait_ge(consts_ready, 4)
            nc.gpsimd.affine_select(out=ga, in_=ga, compare_op=ALU.is_ge, fill=0.0,
                                    base=n - 1, pattern=[[n, P // n], [0, n]], channel_multiplier=-1).then_inc(consts_ready, 1)
            nc.gpsimd.memset(minus_half[:, :], -0.5).then_inc(consts_ready, 1)
            pool.wait_ge(small_loaded, 64)
            pool.wait_ge(consts_ready, 6)

            def low_numerators(g, s):
                pool.wait_ge(ph_done, g * STEPS + s + 1)
                if s >= RING:
                    pool.wait_ge(pv_done, g * STEPS + s - RING + 1)
                nc.gpsimd.tensor_tensor(pl[:, s % RING, :, :], p32[:, s % 2, :, :], ph[:, s % RING, :, :],
                                        ALU.subtract).then_inc(pool_pl_done, 1)

            def shift_residual():
                nc.gpsimd.tensor_tensor(resid_shift[:, :], gn_shift[:, :], bproj[:, :],
                                        ALU.add).then_inc(resid_shifted, 1)

            def affine_form(nb, first=False):
                tt = nc.gpsimd.tensor_tensor
                if not first:
                    pool.wait_ge(xl_done, CT * nb)
                pool.wait_ge(var_eps_done, nb + 1)
                tt(rstd[:, :], var_eps[:, :], minus_half[:, :], ALU.pow).then_inc(affine, 1)
                pool.wait_ge(affine, 4 * nb + 1)
                tt(gn_scale[:, :], rstd[:, :], gam[:, :], ALU.mult).then_inc(affine, 1)
                pool.wait_ge(affine, 4 * nb + 2)
                tt(mean_sc[:, :], gmean[:, :], gn_scale[:, :], ALU.mult).then_inc(affine, 1)
                pool.wait_ge(affine, 4 * nb + 3)
                tt(gn_shift[:, :], bet[:, :], mean_sc[:, :], ALU.subtract).then_inc(affine, 1)
                pool.wait_ge(affine, 4 * nb + 4)
                if not first:
                    pool.wait_ge(k_summed, PAIRS * nb)
                    shift_residual()

            def normalise(c, high=True):
                if high:
                    nc.gpsimd.tensor_scalar(xh[:, c, :], x_sb[:, c, :], gn_scale[:, c:c + 1], gn_shift[:, c:c + 1],
                                            ALU.mult, ALU.add).then_inc(xh_done, 1)
                nc.gpsimd.tensor_scalar(xn32[:, c % 2, :], x_sb[:, c, :], gn_scale[:, c:c + 1], gn_shift[:, c:c + 1],
                                        ALU.mult, ALU.add).then_inc(xn_done, 1)

            def low_normalised(nb, c):
                pool.wait_ge(xh_done, CT * nb + c + 1)
                pool.wait_ge(xn_done, CT * nb + c + 1)
                if c:
                    pool.wait_ge(xl_done, CT * nb + c)
                nc.gpsimd.tensor_tensor(xl[:, c, :], xn32[:, c % 2, :], xh[:, c, :], ALU.subtract).then_inc(xl_done, 1)

            def make_residual(c):
                nc.gpsimd.tensor_scalar(resid[:, c, :], x_sb[:, c, :], gn_scale[:, c:c + 1], resid_shift[:, c:c + 1],
                                        ALU.mult, ALU.add).then_inc(resid_done, 1)

            def finish_half(g, p, u):
                tt = nc.gpsimd.tensor_tensor
                half = slice(u * HALF, (u + 1) * HALF)
                pool.wait_ge(inv_spread[u], SPREAD * (g + 1))
                tt(ah[:, p, half], att32[:, u, :], inv_all[:, u, :], ALU.mult).then_inc(att_hi, 1)
                pool.wait_ge(att_hi, 2 * g + u + 1)
                tt(att32[:, u, :], att32[:, u, :], inv_all[:, u, :], ALU.mult).then_inc(att_scaled, 1)
                pool.wait_ge(att_scaled, 2 * g + u + 1)
                tt(al[:, p, half], att32[:, u, :], ah[:, p, half], ALU.subtract).then_inc(att_lo, 1)

            def turn(b, p, first, last):
                g = b * PAIRS + p
                norm = p == 2 and not last
                if p == 1:
                    if not first:
                        pool.wait_ge(out_ready, CT * b)
                    pool.wait_ge(resid_shifted, b + 1)
                if norm:
                    finish_half(g - 1, 1, 0)
                if p == 0 and not first:
                    finish_half(g - 1, PAIRS - 1, 0)
                    finish_half(g - 1, PAIRS - 1, 1)
                low_numerators(g, POOL_STEPS[0])
                if p > 0 and not norm:
                    finish_half(g - 1, p - 1, 0)
                if norm:
                    affine_form(b + 1)
                    normalise(0)
                low_numerators(g, POOL_STEPS[1])
                if p > 0:
                    finish_half(g - 1, p - 1, 1)
                if norm:
                    normalise(1)
                    low_normalised(b + 1, 0)
                if p == 1:
                    make_residual(0)
                    make_residual(1)
                low_numerators(g, POOL_STEPS[2])
                if norm:
                    low_normalised(b + 1, 1)
                    normalise(2)
                    low_normalised(b + 1, 2)
                if p == 1:
                    make_residual(2)
                    make_residual(3)
                low_numerators(g, POOL_STEPS[3])
                if norm:
                    normalise(3)
                    low_normalised(b + 1, 3)

            affine_form(0, first=True)
            for c in range(CT):
                if c >= 2:
                    pool.wait_ge(xl_done, c - 1)
                normalise(c, high=False)
                low_normalised(0, c)
            pool.wait_ge(bproj_ready, 1)
            shift_residual()
            for p in range(PAIRS):
                turn(0, p, True, False)
            with pool.Fori(1, B - 1) as b:
                for p in range(PAIRS):
                    turn(b, p, False, False)
            for p in range(PAIRS):
                turn(B - 1, p, False, True)
            finish_half(B * PAIRS - 1, PAIRS - 1, 0)
            finish_half(B * PAIRS - 1, PAIRS - 1, 1)

        @block.scalar
        def _(act):
            def q_high(g, p, first=False):
                if not first:
                    act.wait_ge(stacked, STACKED * g)
                    act.wait_ge(max_tile, STEPS * g)
                act.wait_ge(q_summed, g + 1)
                nc.scalar.activation(nat_h[:, 0, :], two_banks(slots[:, 0, :, :]), ACT.Identity,
                                     bias=bq16[:, p:p + 1]).then_inc(q_hi, 1)

            def v_high(b):
                for j in range(KT // 2):
                    act.wait_ge(v_summed, 4 * b + j + 1)
                    nc.scalar.activation(vh[:, 2 * j:2 * j + 2, :], slots[:, (j + 1) % 2, :, :], ACT.Copy).then_inc(v_hi, 1)

            def numerators(g, s):
                n = g * STEPS + s
                act.wait_ge(scored, n + 1)
                if s >= 2:
                    wait_low(act, g, s - 2)
                nc.scalar.activation(p32[:, s % 2, :, :], slots[:, s % 2, :, :], ACT.Exp,
                                     scale=1.0 / MS).then_inc(exp_done, 1)
                act.wait_ge(exp_done, n + 1)
                if s >= RING:
                    act.wait_ge(pv_done, n - RING + 1)
                nc.scalar.activation(ph[:, s % RING, :, :], p32[:, s % 2, :, :], ACT.Copy).then_inc(ph_done, 1)

            def read_half(g, u, first=False):
                act.wait_ge(pv_done, g * STEPS + (u + 1) * KT)
                if not first:
                    act.wait_ge(att_lo, 2 * g)
                nc.scalar.activation(att32[:, u, :], acc[:, :], ACT.Copy)
                nc.scalar.activation(sums_sb[:, u, :], sums[:, 0:QUARTER], ACT.Copy).then_inc(half_read, 1)

            def turn(b, p, first, last):
                g = b * PAIRS + p
                has_next = not (last and p == PAIRS - 1)
                if not (first and p == 0):
                    read_half(g - 1, 1, first=first and p == 1)
                if has_next:
                    q_high(g + 1, (p + 1) % PAIRS)
                if p == 0 and not first:
                    v_high(b)
                numerators(g, 0)
                numerators(g, 1)
                for s in range(2, STEPS):
                    numerators(g, s)
                    if s == KT + 1:
                        read_half(g, 0, first=first and p == 0)

            for c in range(CT):
                act.wait_ge(w_loaded[c % 2], 32 * (c // 2 + 1))
                nc.scalar.activation(wq_h[:, c, :], raw_w(c)[0], ACT.Copy, scale=WS).then_inc(w_split_h, 1)
                nc.scalar.activation(wp_h[:, c, :], raw_w(c)[1], ACT.Copy, scale=WS).then_inc(w_split_h, 1)
                if c == 0:
                    act.wait_ge(affine, 4)
                nc.scalar.activation(xh[:, c, :], x_sb[:, c, :], ACT.Identity, bias=gn_shift[:, c:c + 1],
                                     scale=gn_scale[:, c:c + 1]).then_inc(xh_done, 1)
            act.wait_ge(bias_ready, 1)
            q_high(0, 0, first=True)
            v_high(0)
            act.wait_ge(w_split_l, 2 * CT)
            for p in range(PAIRS):
                turn(0, p, True, False)
            with act.Fori(1, B - 1) as b:
                for p in range(PAIRS):
                    turn(b, p, False, False)
            for p in range(PAIRS):
                turn(B - 1, p, False, True)
            read_half(B * PAIRS - 1, 1)

        @block.vector
        def _(dve):
            nc.vector.memset(ones[:, :], 1.0).then_inc(rows_ready, 1)
            nc.vector.memset(k_main[D:D + 1, :, :, :], MS).then_inc(rows_ready, 1)
            dve.wait_ge(small_loaded, 64)
            nc.vector.tensor_scalar(bq16[:, :], bias_raw[:, :], WS, None, ALU.mult).then_inc(bias_ready, 1)
            dve.wait_ge(bias_ready, 1)
            nc.vector.tensor_copy(bv_h[:, :], bq16[:, 2 * CT:3 * CT]).then_inc(bv_split, 1)
            dve.wait_ge(bv_split, 1)
            nc.vector.tensor_tensor(bv_l[:, :], bq16[:, 2 * CT:3 * CT], bv_h[:, :], ALU.subtract).then_inc(bv_split, 1)

            def gn_stats(nb, c):
                dve.wait_ge(x_loaded[c], 16 * (nb + 1))
                for a in range(2):
                    nc.vector.bn_stats(stats[:, c, a, :], x_sb[:, c, a * HALF:(a + 1) * HALF]).then_inc(stats_done, 1)

            def gn_aggregate():
                for c in range(CT):
                    nc.vector.bn_aggr(mv[:, c, :], stats[:, c, :, :].rearrange("p a s -> p (a s)")).then_inc(aggr_done, 1)

            def gn_center(nb):
                dve.wait_ge(gmean_summed, nb + 1)
                nc.vector.tensor_copy(gmean[:, :], acc[:, 0:CT]).then_inc(gmean_copied, 1)
                dve.wait_ge(gmean_copied, nb + 1)
                nc.vector.tensor_tensor(dev[:, :], mv[:, :, 0], gmean[:, :], ALU.subtract).then_inc(dev_done, 1)
                dve.wait_ge(dev_done, nb + 1)
                nc.vector.tensor_tensor(dev2[:, :], dev[:, :], dev[:, :], ALU.mult).then_inc(dev2_done, 1)
                dve.wait_ge(dev2_done, nb + 1)
                nc.vector.tensor_tensor(chan_var[:, :], dev2[:, :], mv[:, :, 1], ALU.add).then_inc(chan_var_done, 1)

            def gn_var(nb):
                dve.wait_ge(gvar_summed, nb + 1)
                nc.vector.tensor_scalar(var_eps[:, :], acc[:, 0:CT], EPS, None, ALU.add).then_inc(var_eps_done, 1)

            def k_high(g, p):
                dve.wait_ge(k_summed, g + 1)
                nc.vector.tensor_scalar(nat_h[:, 1, :], two_banks(side[:, :, :]), bq16[:, CT + p:CT + p + 1], None,
                                        ALU.add).then_inc(k_hi, 1)

            def qk_low(g, i, p):
                dve.wait_ge(k_hi if i else q_hi, g + 1)
                src = slots[:, 0, :, :] if i == 0 else side[:, :, :]
                nc.vector.scalar_tensor_tensor(
                    out=nat_l[:, i, :], in0=two_banks(src), scalar=bq16[:, i * CT + p:i * CT + p + 1],
                    in1=nat_h[:, i, :], op0=ALU.add, op1=ALU.subtract).then_inc(qk_lo, 1)

            def v_low(b, j):
                dve.wait_ge(v_hi, 4 * b + j + 1)
                nc.vector.tensor_tensor(vl[:, 2 * j:2 * j + 2, :], slots[:, (j + 1) % 2, :, :], vh[:, 2 * j:2 * j + 2, :],
                                        ALU.subtract).then_inc(v_lo, 1)

            def max_reduce(g, m):
                dve.wait_ge(max_tile, g * STEPS + m + 1)
                nc.vector.tensor_reduce(max_part[:, m // 2, m % 2, :], side[:, :, :], axis=AX.X,
                                        op=ALU.max).then_inc(max_reduced, 1)

            def max_combine(g):
                dve.wait_ge(max_reduced, (g + 1) * STEPS)
                nc.vector.tensor_tensor(max_all[:, :, :].rearrange("p h n -> p n h"), max_part[:, :, 0, :],
                                        max_part[:, :, 1, :], ALU.max).then_inc(max_combined, 1)

            def max_finish(g, first=False):
                dve.wait_ge(max_turned, g + 1)
                if not first:
                    dve.wait_ge(max_stacked, 32 * g)
                nc.vector.tensor_scalar(max_row[:, :], side[0:2 * KT, 1, 0:P], -1.0 / MS, None,
                                        ALU.mult).then_inc(max_scaled, 1)

            def low_numerators(g, s):
                n = g * STEPS + s
                dve.wait_ge(ph_done, n + 1)
                if s >= RING:
                    dve.wait_ge(pv_done, n - RING + 1)
                nc.vector.tensor_tensor(pl[:, s % RING, :, :], p32[:, s % 2, :, :], ph[:, s % RING, :, :],
                                        ALU.subtract).then_inc(pl_done, 1)

            def invert(g, u, first=False):
                dve.wait_ge(half_read, 2 * g + u + 1)
                if not first:
                    dve.wait_ge(inv_spread[u], SPREAD * g)
                nc.vector.reciprocal(inv_sum[:, u, :], sums_sb[:, u, :]).then_inc(inv_done, 1)

            def project(b, first=False):
                for j in range(CT):
                    dve.wait_ge(proj_summed, CT * b + j + 1)
                    if j >= 2 or not first:
                        dve.wait_ge(out_stored[j % 2], 16 * (CT // 2 * b + j // 2))
                    if j == 0:
                        dve.wait_ge(resid_done, CT * (b + 1))
                    nc.vector.scalar_tensor_tensor(
                        out=stage[:, j % 2, :], in0=two_banks(slots[:, j % 2, :, :]),
                        scalar=1.0 / (WS * WS), in1=resid[:, j, :], op0=ALU.mult, op1=ALU.add).then_inc(out_ready, 1)

            def turn(b, p, first, last):
                g = b * PAIRS + p
                has_next = not (last and p == PAIRS - 1)
                start = first and p == 0
                norm = p == 2 and not last
                max_reduce(g, STEPS - 3)
                if norm:
                    gn_stats(b + 1, 0)
                max_reduce(g, STEPS - 2)
                if norm:
                    gn_stats(b + 1, 1)
                max_reduce(g, STEPS - 1)
                max_combine(g)
                max_finish(g, first=start)
                if norm:
                    gn_stats(b + 1, 2)
                if has_next:
                    qk_low(g + 1, 0, (p + 1) % PAIRS)
                if norm:
                    gn_stats(b + 1, 3)
                if not start and not norm:
                    invert(g - 1, 0, first=first and p == 1)
                if norm:
                    dve.wait_ge(stats_done, 2 * CT * (b + 2))
                if not start:
                    invert(g - 1, 1, first=first and p == 1)
                if norm:
                    gn_aggregate()
                if p == 0 and not start:
                    for j in range(KT // 2):
                        v_low(b, j)
                    if not first:
                        project(b - 1, first=isinstance(b, int) and b == 1)
                if norm:
                    gn_center(b + 1)
                low_numerators(g, 0)
                if norm:
                    gn_var(b + 1)
                if has_next:
                    k_high(g + 1, (p + 1) % PAIRS)
                    qk_low(g + 1, 1, (p + 1) % PAIRS)
                for s in range(2, STEPS):
                    if has_next:
                        if s == 2:
                            max_reduce(g + 1, 0)
                        elif s != 4:
                            max_reduce(g + 1, max(s - 3, 1))
                    if s not in POOL_STEPS:
                        low_numerators(g, s)
                    if s == POOL_STEPS[-1] and ((p == 1 and not last) or not has_next):
                        invert(g, 0)

            for c in range(CT):
                gn_stats(0, c)
            dve.wait_ge(stats_done, 2 * CT)
            gn_aggregate()
            gn_center(0)
            gn_var(0)
            for c in range(CT):
                dve.wait_ge(w_split_h, 2 * c + 2)
                nc.vector.scalar_tensor_tensor(out=wq_l[:, c, :], in0=raw_w(c)[0], scalar=WS, in1=wq_h[:, c, :],
                                               op0=ALU.mult, op1=ALU.subtract).then_inc(w_split_l, 1)
                nc.vector.scalar_tensor_tensor(out=wp_l[:, c, :], in0=raw_w(c)[1], scalar=WS, in1=wp_h[:, c, :],
                                               op0=ALU.mult, op1=ALU.subtract).then_inc(w_split_l, 1)
            dve.wait_ge(bv_summed, 1)
            nc.vector.scalar_tensor_tensor(out=bproj[:, :], in0=acc[:, 0:CT], scalar=1.0 / (WS * WS), in1=bproj_raw[:, :],
                                           op0=ALU.mult, op1=ALU.add).then_inc(bproj_ready, 1)
            qk_low(0, 0, 0)
            k_high(0, 0)
            qk_low(0, 1, 0)
            for m in range(STEPS - 3):
                max_reduce(0, m)
                if m and m % 3 == 0:
                    v_low(0, m // 3 - 1)
            for p in range(PAIRS):
                turn(0, p, True, False)
            with dve.Fori(1, B - 1) as b:
                for p in range(PAIRS):
                    turn(b, p, False, False)
            for p in range(PAIRS):
                turn(B - 1, p, False, True)
            invert(B * PAIRS - 1, 1)
            project(B - 1)

        @block.tensor
        def _(pe):
            mm = nc.tensor.matmul
            pe.wait_ge(consts_ready, 6)
            pe.wait_ge(rows_ready, 2)

            def gn_group_mean(nb):
                pe.wait_ge(aggr_done, CT * (nb + 1))
                mm(acc[:, 0:CT], group_avg[:, :], mv[:, :, 0], start=True, stop=True).then_inc(gmean_summed, 1)

            def gn_group_var(nb):
                pe.wait_ge(chan_var_done, nb + 1)
                mm(acc[:, 0:CT], group_avg[:, :], chan_var[:, :], start=True, stop=True).then_inc(gvar_summed, 1)

            def three(bank, parts, at=None):
                last = None
                terms = [(w[i], m[j]) for w, m in parts for i, j in ((0, 0), (0, 1), (1, 0))]
                for t, (w, m) in enumerate(terms):
                    if at and t in at:
                        at[t]()
                    last = mm(bank, w, m, start=t == 0, stop=t == len(terms) - 1)
                return last

            def qk_project(i, a, p, at=None):
                cols = slice(i * C + p * P, i * C + (p + 1) * P)
                half = slice(a * HALF, (a + 1) * HALF)
                bank = slots[:, 0, a, :] if i == 0 else side[:, a, :]
                last = three(bank, [((wq_h[:, c, cols], wq_l[:, c, cols]), (xh[:, c, half], xl[:, c, half]))
                                    for c in range(CT)], at)
                if a == 1:
                    last.then_inc(k_summed if i else q_summed, 1)

            def v_project(b, free, at=None):
                for j in range(KT // 2):
                    if j < 2:
                        free((j + 1) % 2)
                    else:
                        pe.wait_ge(v_lo, 4 * b + j - 1)
                    for a in range(2):
                        pos = slice((2 * j + a) * P, (2 * j + a + 1) * P)
                        t0 = (2 * j + a) * 3 * CT
                        last = three(slots[:, (j + 1) % 2, a, :], [((xh[:, c, pos], xl[:, c, pos]),
                                                              (wq_h[:, c, 2 * C:3 * C], wq_l[:, c, 2 * C:3 * C]))
                                                             for c in range(CT)],
                                     {t: at[t0 + t] for t in range(3 * CT) if t0 + t in at} if at else None)
                    last.then_inc(v_summed, 1)

            def max_pass(g, m):
                if m == 0:
                    pe.wait_ge(qk_lo, 2 * g + 2)
                else:
                    pe.wait_ge(max_reduced, g * STEPS + m)
                q0, k0 = (m // 2) * P, (m % 2) * HALF
                for h in range(2):
                    last = mm(side[:, h, :], nat_h[h * D:(h + 1) * D, 0, q0:q0 + P],
                              nat_h[h * D:(h + 1) * D, 1, k0:k0 + HALF], start=True, stop=True)
                last.then_inc(max_tile, 1)

            def max_turn(g):
                pe.wait_ge(max_combined, g + 1)
                nc.tensor.transpose(side[0:2 * KT, 1, 0:P], max_all[:, :, :].rearrange("p h n -> p (h n)"),
                                    ident[:, :]).then_inc(max_turned, 1)

            def score(g, par, s):
                if s >= 2:
                    pe.wait_ge(exp_done, g * STEPS + s - 1)
                u, st = s // KT, s % KT
                keys, queries = slice(st * P, (st + 1) * P), slice(u * HALF, (u + 1) * HALF)
                for h in range(2):
                    mm(slots[:, s % 2, h, :], k_cross[:, par, h, keys], q_cross[:, par, h, queries], start=True, stop=False)
                    last = mm(slots[:, s % 2, h, :], k_main[:, par, h, keys], q_main[:, par, h, queries], start=False, stop=True)
                last.then_inc(scored, 1)

            def weigh(g, p, s, low):
                u, st = s // KT, s % KT
                if low:
                    wait_low(pe, g, s)
                else:
                    pe.wait_ge(ph_done, g * STEPS + s + 1)
                for i, (v, m) in enumerate(((vh, pl),) if low else ((vh, ph), (vl, ph))):
                    for h in range(2):
                        c0 = p * P + h * D
                        mm(acc[h * D:(h + 1) * D, :], v[:, st, c0:c0 + D], m[:, s % RING, h, :],
                           start=st == 0 and i == 0 and not low, stop=st == KT - 1 and low)

            def add_up(s):
                st = s % KT
                for i, m in enumerate((ph, pl)):
                    for h in range(2):
                        for q in range(2):
                            row = 32 * (2 * h + q)
                            last = mm(sums[row:row + 32, 0:QUARTER], ones[:, 0:32],
                                      m[:, s % RING, h, q * QUARTER:(q + 1) * QUARTER],
                                      start=st == 0 and i == 0, stop=st == KT - 1 and i == 1)
                last.then_inc(pv_done, 1)

            def project(b, free):
                for j in range(CT):
                    if j < 2:
                        free(j)
                    else:
                        pe.wait_ge(out_ready, CT * b + j - 1)
                    cols = slice(j * P, (j + 1) * P)
                    for a in range(2):
                        half = slice(a * HALF, (a + 1) * HALF)
                        at = {3 * (PAIRS - 1): lambda a=a: pe.wait_ge(att_lo, 2 * PAIRS * (b + 1) - 1 + a)}
                        last = three(slots[:, j % 2, a, :], [((wp_h[:, c, cols], wp_l[:, c, cols]),
                                                              (ah[:, c, half], al[:, c, half])) for c in range(PAIRS)],
                                     at if j == 0 else None)
                    last.then_inc(proj_summed, 1)

            def turn(b, p, first, last):
                g = b * PAIRS + p
                has_next = not (last and p == PAIRS - 1)
                start = first and p == 0
                norm = p == 2 and not last
                if has_next:
                    if not start:
                        pe.wait_ge(exp_done, STEPS * g - 1)
                    at = {}
                    if p == PAIRS - 1:
                        at = {3 * c: lambda c=c: pe.wait_ge(xl_done, CT * (b + 1) + c + 1) for c in range(CT)}
                    at[7] = lambda: max_pass(g, STEPS - 3)
                    qk_project(0, 0, (p + 1) % PAIRS, at)
                else:
                    max_pass(g, STEPS - 3)
                if not start:
                    weigh(g - 1, (p - 1) % PAIRS, STEPS - 2, low=False)
                    weigh(g - 1, (p - 1) % PAIRS, STEPS - 1, low=False)
                max_pass(g, STEPS - 2)
                if not start:
                    weigh(g - 1, (p - 1) % PAIRS, STEPS - 2, low=True)
                    weigh(g - 1, (p - 1) % PAIRS, STEPS - 1, low=True)
                    add_up(STEPS - 2)
                    add_up(STEPS - 1)
                if has_next:
                    qk_project(0, 1, (p + 1) % PAIRS,
                               at={4: lambda: max_pass(g, STEPS - 1), 11: lambda: max_turn(g)})
                else:
                    max_pass(g, STEPS - 1)
                    max_turn(g)
                if p == 0 and not start:
                    def slot_for_v(j):
                        if j == 0:
                            pe.wait_ge(qk_lo, 2 * (g + 1) + 1)
                        else:
                            pe.wait_ge(exp_done, STEPS * g)
                    v_project(b, slot_for_v)
                if has_next:
                    pe.wait_ge(max_reduced, STEPS * (g + 1))
                    qk_project(1, 0, (p + 1) % PAIRS)
                if p == 0 and not first:
                    project(b - 1, lambda j: pe.wait_ge(v_lo, 4 * b + 4 - j))
                if p == 0:
                    if first:
                        pe.wait_ge(qk_lo, 3)
                    else:
                        pe.wait_ge(out_ready, CT * b - 1)
                elif has_next:
                    pe.wait_ge(qk_lo, 2 * (g + 1) + 1)
                    pe.wait_ge(exp_done, STEPS * g)
                else:
                    pe.wait_ge(exp_done, STEPS * g)

                def first_step():
                    pe.wait_ge(stacked, STACKED * (g + 1))
                    pe.wait_ge(max_stacked, 32 * (g + 1))
                    score(g, p % 2, 0)

                def second_step():
                    if p == 0 and not first:
                        pe.wait_ge(out_ready, CT * b)
                    score(g, p % 2, 1)
                    if norm:
                        pe.wait_ge(half_read, 2 * g)
                        gn_group_mean(b + 1)

                if has_next:
                    pe.wait_ge(max_scaled, g + 1)
                    qk_project(1, 1, (p + 1) % PAIRS, at={4: first_step, 8: second_step})
                else:
                    first_step()
                    second_step()
                for s in range(2, STEPS, 2):
                    score(g, p % 2, s)
                    if has_next and s > 2:
                        max_pass(g + 1, s - 3)
                    if norm and s == 2:
                        gn_group_var(b + 1)
                    score(g, p % 2, s + 1)
                    if norm and s == 2:
                        pe.wait_ge(var_eps_done, b + 2)
                    if s == 2 and not start:
                        pe.wait_ge(half_read, 2 * g)
                    if s == KT + 2:
                        pe.wait_ge(half_read, 2 * g + 1)
                    weigh(g, p, s - 2, low=False)
                    weigh(g, p, s - 1, low=False)
                    if has_next and s > 2:
                        max_pass(g + 1, s - 2)
                    weigh(g, p, s - 2, low=True)
                    if has_next and s == 2:
                        max_pass(g + 1, 0)
                    weigh(g, p, s - 1, low=True)
                    add_up(s - 2)
                    add_up(s - 1)

            gn_group_mean(0)
            gn_group_var(0)
            pe.wait_ge(w_split_l, 2 * CT)
            pe.wait_ge(var_eps_done, 1)
            pe.wait_ge(bv_split, 2)
            for j in range(CT):
                cols = slice(j * P, (j + 1) * P)
                last = three(acc[:, j:j + 1], [((wp_h[:, c, cols], wp_l[:, c, cols]),
                                                (bv_h[:, c:c + 1], bv_l[:, c:c + 1])) for c in range(CT)])
            last.then_inc(bv_summed, 1)
            for i in range(2):
                for a in range(2):
                    qk_project(i, a, 0, at={3 * c: lambda c=c: pe.wait_ge(xl_done, c + 1) for c in range(CT)}
                               if i == a == 0 else None)
            v_project(0, lambda j: None, at={8 * m: lambda m=m: max_pass(0, m) for m in range(STEPS - 4)})
            max_pass(0, STEPS - 4)
            pe.wait_ge(v_lo, 4)
            pe.wait_ge(bproj_ready, 1)
            for p in range(PAIRS):
                turn(0, p, True, False)
            with pe.Fori(1, B - 1) as b:
                for p in range(PAIRS):
                    turn(b, p, False, False)
            for p in range(PAIRS):
                turn(B - 1, p, False, True)
            g_end = B * PAIRS
            for low in (False, True):
                for s in (STEPS - 2, STEPS - 1):
                    weigh(g_end - 1, PAIRS - 1, s, low)
            for s in (STEPS - 2, STEPS - 1):
                add_up(s)
            project(B - 1, lambda j: pe.wait_ge(exp_done, STEPS * g_end - 1 + j))


def kernel(**inputs):
    import numpy as _np
    import concourse.bacc as _bacc
    from concourse import mybir as _mybir
    from concourse.bass_utils import run_bass_kernel_spmd as _run

    nc = _bacc.Bacc("TRN2", target_bir_lowering=False, num_devices=1)
    f = {k: _np.asarray(v) for k, v in inputs.items()}
    laid_out = {
        "x": f["x"].reshape(B, C, T),
        "gamma": f["L0_conv_gamma"].reshape(-1, P).T,
        "beta": f["L0_conv_beta"].reshape(-1, P).T,
        "w_qkv_t": _np.ascontiguousarray(f["L0_conv_w_qkv"].T),
        "b_qkv": f["L0_conv_b_qkv"].reshape(-1, P).T,
        "w_proj_t": _np.ascontiguousarray(f["L0_conv_w_proj"].T),
        "b_proj": f["L0_conv_b_proj"].reshape(-1, P).T,
    }
    arrays, args = {}, []
    for name, a in laid_out.items():
        a = _np.ascontiguousarray(a)
        arrays[name] = a
        args.append(nc.dram_tensor(name, a.shape, _mybir.dt.from_np(a.dtype), kind="ExternalInput").ap())
    y = nc.dram_tensor("y", (B, C, T), _mybir.dt.float32, kind="ExternalOutput").ap()
    attention_block_kernel(nc, *args, y)
    r = _run(nc, [arrays], core_ids=[0])
    return r.results[0]["y"].reshape(f["x"].shape)
```
